# Optimizing a Trainium2 kernel written in Bass

```python
import numpy as np
import jax
import jax.numpy as jnp

def _softmax(x, axis=-1):
    return jax.nn.softmax(x, axis=axis)

def _gelu(x):
    return jax.nn.gelu(x, approximate=True)

def _silu(x):
    return jax.nn.silu(x)

def _sigmoid(x):
    return jax.nn.sigmoid(x)

def _layernorm(x, axis=-1, eps=1e-05):
    m = jnp.mean(x, axis=axis, keepdims=True)
    v = jnp.var(x, axis=axis, keepdims=True)
    return (x - m) / jnp.sqrt(v + eps)

def _scatter_add(tgt, idx, src, axis=0):
    return tgt.at[idx].add(src)

def _segment_sum(src, seg, n):
    return jax.ops.segment_sum(src, seg, n)
kernel_name = 'mk_gnn_resnorm_d2_gnn_r8_4030f5'

def setup_inputs(seed: int=0):
    np.random.seed(seed)
    _w = jnp.asarray

    def _rec_inputs():
        import jax
        import jax.numpy as jnp
        _gk = jax.random.key(seed)
        x = -0.0005121 + 1.001 * jax.random.normal(jax.random.fold_in(_gk, 1), (12500, 32), jnp.float32)
        src = jax.random.randint(jax.random.fold_in(_gk, 2), (400000,), 0, 12500, jnp.int32)
        dst = jax.random.randint(jax.random.fold_in(_gk, 3), (400000,), 0, 12500, jnp.int32)
        _o = jnp.argsort(dst, stable=True)
        src = src[_o]
        dst = dst[_o]
        edge_attr_16 = 0.000254156 + 0.999948 * jax.random.normal(jax.random.fold_in(_gk, 11), (400000, 16), jnp.float32)
        edge_attr_3 = jax.random.uniform(jax.random.fold_in(_gk, 12), (400000, 3), jnp.float32, 0.0, 1)
        return (x, src, dst, edge_attr_16, edge_attr_3)
    x, src, dst, edge_attr_16, edge_attr_3 = _rec_inputs()

    def _L0_gnn_setup():
        import jax, jax.numpy as jnp
        import numpy as np
        N = 12500
        E = 200000
        CIN = 32
        COUT = 32
        K = 5
        EPS = 1e-15
        BN_EPS = 1e-05

        def gmm_conv(x, edge_index, edge_attr, g, mu, sigma, root, bias):
            src, dst = (edge_index[0], edge_index[1])
            n = x.shape[0]
            k = mu.shape[0]
            cout = root.shape[1]
            xg = (x @ g).reshape(n, k, cout)
            xj = xg[src]
            d = edge_attr[:, None, :] - mu[None, :, :]
            w = jnp.exp(-0.5 * jnp.sum(d * d / (EPS + sigma[None] ** 2), axis=-1))
            msg = jnp.einsum('eko,ek->eo', xj, w)
            agg = jax.ops.segment_sum(msg, dst, num_segments=n)
            cnt = jax.ops.segment_sum(jnp.ones((msg.shape[0],), x.dtype), dst, num_segments=n)
            agg = agg / jnp.clip(cnt, 1.0)[:, None]
            return agg + x @ root + bias

        def batch_norm(x, gamma, beta):
            m = x.mean(0)
            v = x.var(0)
            return (x - m) * jax.lax.rsqrt(v + BN_EPS) * gamma + beta
        key = jax.random.key(seed)
        ks = jax.random.split(key, 12)
        p = lambda k, s, sc=0.1: jax.random.normal(k, s, jnp.float32) * sc
        return {'x': jax.random.normal(ks[0], (N, CIN), jnp.float32), 'edge_index': jax.random.randint(ks[1], (2, E), 0, N, jnp.int32), 'edge_attr': jax.random.uniform(ks[2], (E, 3), jnp.float32), 'g1': p(ks[3], (CIN, K * COUT)), 'mu1': p(ks[4], (K, 3), 1.0), 'sigma1': jnp.ones((K, 3), jnp.float32), 'root1': p(ks[5], (CIN, COUT)), 'b1': jnp.zeros((COUT,), jnp.float32), 'gam1': jnp.ones((COUT,), jnp.float32), 'bet1': jnp.zeros((COUT,), jnp.float32), 'g2': p(ks[6], (COUT, K * COUT)), 'mu2': p(ks[7], (K, 3), 1.0), 'sigma2': jnp.ones((K, 3), jnp.float32), 'root2': p(ks[8], (COUT, COUT)), 'b2': jnp.zeros((COUT,), jnp.float32), 'gam2': jnp.ones((COUT,), jnp.float32), 'bet2': jnp.zeros((COUT,), jnp.float32), 'gs': p(ks[9], (CIN, 1 * COUT)), 'mus': p(ks[10], (1, 3), 1.0), 'sigmas': jnp.ones((1, 3), jnp.float32), 'roots': p(ks[11], (CIN, COUT)), 'bs': jnp.zeros((COUT,), jnp.float32), 'gams': jnp.ones((COUT,), jnp.float32), 'bets': jnp.zeros((COUT,), jnp.float32)}
    _L0_gnn_all = _L0_gnn_setup()
    _L0_gnn_in = {k: v for k, v in _L0_gnn_all.items() if k in ('g1', 'mu1', 'sigma1', 'root1', 'b1', 'gam1', 'bet1', 'g2', 'mu2', 'sigma2', 'root2', 'b2', 'gam2', 'bet2', 'gs', 'mus', 'sigmas', 'roots', 'bs', 'gams', 'bets')}
    del _L0_gnn_all

    def _L1_gnn_setup():
        import jax, jax.numpy as jnp
        import numpy as np
        N_NODES = 6250
        N_EDGES = 100000
        NODE_D, EDGE_D = (32, 16)
        FLOW_IN, FLOW_H, FLOW_OUT = (2 * NODE_D + EDGE_D, 64, 64)
        NODE_H, NODE_OUT = (64, 32)

        def _mlp(h, W1, b1, W2, b2):
            h = jax.nn.relu(h @ W1 + b1)
            return h @ W2 + b2
        key = jax.random.key(seed)
        ks = jax.random.split(key, 8)
        return {'x': jax.random.normal(ks[0], (N_NODES, NODE_D), dtype=jnp.float32), 'edge_index': jax.random.randint(ks[1], (2, N_EDGES), 0, N_NODES, dtype=jnp.int64), 'edge_attr': jax.random.normal(ks[2], (N_EDGES, EDGE_D), dtype=jnp.float32), 'Wf1': jax.random.normal(ks[3], (FLOW_IN, FLOW_H), dtype=jnp.float32) * (1.0 / np.sqrt(FLOW_IN)), 'bf1': jnp.zeros((FLOW_H,), dtype=jnp.float32), 'Wf2': jax.random.normal(ks[4], (FLOW_H, FLOW_OUT), dtype=jnp.float32) * (1.0 / np.sqrt(FLOW_H)), 'bf2': jnp.zeros((FLOW_OUT,), dtype=jnp.float32), 'Wn1': jax.random.normal(ks[5], (FLOW_OUT, NODE_H), dtype=jnp.float32) * (1.0 / np.sqrt(FLOW_OUT)), 'bn1': jnp.zeros((NODE_H,), dtype=jnp.float32), 'Wn2': jax.random.normal(ks[6], (NODE_H, NODE_OUT), dtype=jnp.float32) * (1.0 / np.sqrt(NODE_H)), 'bn2': jnp.zeros((NODE_OUT,), dtype=jnp.float32)}
    _L1_gnn_all = _L1_gnn_setup()
    _L1_gnn_in = {k: v for k, v in _L1_gnn_all.items() if k in ('Wf1', 'bf1', 'Wf2', 'bf2', 'Wn1', 'bn1', 'Wn2', 'bn2')}
    del _L1_gnn_all
    return {'x': x, 'src': src, 'dst': dst, 'edge_attr_16': edge_attr_16, 'edge_attr_3': edge_attr_3, 'L0_gnn_g1': _L0_gnn_in['g1'], 'L0_gnn_mu1': _L0_gnn_in['mu1'], 'L0_gnn_sigma1': _L0_gnn_in['sigma1'], 'L0_gnn_root1': _L0_gnn_in['root1'], 'L0_gnn_b1': _L0_gnn_in['b1'], 'L0_gnn_gam1': _L0_gnn_in['gam1'], 'L0_gnn_bet1': _L0_gnn_in['bet1'], 'L0_gnn_g2': _L0_gnn_in['g2'], 'L0_gnn_mu2': _L0_gnn_in['mu2'], 'L0_gnn_sigma2': _L0_gnn_in['sigma2'], 'L0_gnn_root2': _L0_gnn_in['root2'], 'L0_gnn_b2': _L0_gnn_in['b2'], 'L0_gnn_gam2': _L0_gnn_in['gam2'], 'L0_gnn_bet2': _L0_gnn_in['bet2'], 'L0_gnn_gs': _L0_gnn_in['gs'], 'L0_gnn_mus': _L0_gnn_in['mus'], 'L0_gnn_sigmas': _L0_gnn_in['sigmas'], 'L0_gnn_roots': _L0_gnn_in['roots'], 'L0_gnn_bs': _L0_gnn_in['bs'], 'L0_gnn_gams': _L0_gnn_in['gams'], 'L0_gnn_bets': _L0_gnn_in['bets'], 'L1_gnn_Wf1': _L1_gnn_in['Wf1'], 'L1_gnn_bf1': _L1_gnn_in['bf1'], 'L1_gnn_Wf2': _L1_gnn_in['Wf2'], 'L1_gnn_bf2': _L1_gnn_in['bf2'], 'L1_gnn_Wn1': _L1_gnn_in['Wn1'], 'L1_gnn_bn1': _L1_gnn_in['bn1'], 'L1_gnn_Wn2': _L1_gnn_in['Wn2'], 'L1_gnn_bn2': _L1_gnn_in['bn2']}

def reference(x, src, dst, edge_attr_16, edge_attr_3, L0_gnn_g1, L0_gnn_mu1, L0_gnn_sigma1, L0_gnn_root1, L0_gnn_b1, L0_gnn_gam1, L0_gnn_bet1, L0_gnn_g2, L0_gnn_mu2, L0_gnn_sigma2, L0_gnn_root2, L0_gnn_b2, L0_gnn_gam2, L0_gnn_bet2, L0_gnn_gs, L0_gnn_mus, L0_gnn_sigmas, L0_gnn_roots, L0_gnn_bs, L0_gnn_gams, L0_gnn_bets, L1_gnn_Wf1, L1_gnn_bf1, L1_gnn_Wf2, L1_gnn_bf2, L1_gnn_Wn1, L1_gnn_bn1, L1_gnn_Wn2, L1_gnn_bn2):
    import jax
    import jax.numpy as jnp

    def _L0_gnn_ref(x, edge_index, edge_attr, g1, mu1, sigma1, root1, b1, gam1, bet1, g2, mu2, sigma2, root2, b2, gam2, bet2, gs, mus, sigmas, roots, bs, gams, bets):
        import jax, jax.numpy as jnp
        import numpy as np
        N = 12500
        E = 200000
        CIN = 32
        COUT = 32
        K = 5
        EPS = 1e-15
        BN_EPS = 1e-05

        def gmm_conv(x, edge_index, edge_attr, g, mu, sigma, root, bias):
            src, dst = (edge_index[0], edge_index[1])
            n = x.shape[0]
            k = mu.shape[0]
            cout = root.shape[1]
            xg = (x @ g).reshape(n, k, cout)
            xj = xg[src]
            d = edge_attr[:, None, :] - mu[None, :, :]
            w = jnp.exp(-0.5 * jnp.sum(d * d / (EPS + sigma[None] ** 2), axis=-1))
            msg = jnp.einsum('eko,ek->eo', xj, w)
            agg = jax.ops.segment_sum(msg, dst, num_segments=n)
            cnt = jax.ops.segment_sum(jnp.ones((msg.shape[0],), x.dtype), dst, num_segments=n)
            agg = agg / jnp.clip(cnt, 1.0)[:, None]
            return agg + x @ root + bias

        def batch_norm(x, gamma, beta):
            m = x.mean(0)
            v = x.var(0)
            return (x - m) * jax.lax.rsqrt(v + BN_EPS) * gamma + beta
        h = jax.nn.elu(batch_norm(gmm_conv(x, edge_index, edge_attr, g1, mu1, sigma1, root1, b1), gam1, bet1))
        h = batch_norm(gmm_conv(h, edge_index, edge_attr, g2, mu2, sigma2, root2, b2), gam2, bet2)
        s = batch_norm(gmm_conv(x, edge_index, edge_attr, gs, mus, sigmas, roots, bs), gams, bets)
        return jax.nn.elu(h + s)

    def _L1_gnn_ref(x, edge_index, edge_attr, Wf1, bf1, Wf2, bf2, Wn1, bn1, Wn2, bn2):
        import jax, jax.numpy as jnp
        import numpy as np
        N_NODES = 6250
        N_EDGES = 100000
        NODE_D, EDGE_D = (32, 16)
        FLOW_IN, FLOW_H, FLOW_OUT = (2 * NODE_D + EDGE_D, 64, 64)
        NODE_H, NODE_OUT = (64, 32)

        def _mlp(h, W1, b1, W2, b2):
            h = jax.nn.relu(h @ W1 + b1)
            return h @ W2 + b2
        past, future = (edge_index[0], edge_index[1])
        x_p = x[past]
        x_f = x[future]
        flow_fwd = jnp.concatenate([x_f, x_p, edge_attr], axis=1)
        flow_bwd = jnp.concatenate([x_p, x_f, edge_attr], axis=1)
        flow_total_in = jnp.concatenate([flow_fwd, flow_bwd], axis=0)
        flow_processed = _mlp(flow_total_in, Wf1, bf1, Wf2, bf2)
        dest = jnp.concatenate([future, past], axis=0)
        flow_total = jax.ops.segment_sum(flow_processed, dest, num_segments=x.shape[0])
        return _mlp(flow_total, Wn1, bn1, Wn2, bn2)
    edge_index = jnp.stack([src, dst])
    x = _layernorm(x + _L0_gnn_ref(x, edge_index, edge_attr_3, L0_gnn_g1, L0_gnn_mu1, L0_gnn_sigma1, L0_gnn_root1, L0_gnn_b1, L0_gnn_gam1, L0_gnn_bet1, L0_gnn_g2, L0_gnn_mu2, L0_gnn_sigma2, L0_gnn_root2, L0_gnn_b2, L0_gnn_gam2, L0_gnn_bet2, L0_gnn_gs, L0_gnn_mus, L0_gnn_sigmas, L0_gnn_roots, L0_gnn_bs, L0_gnn_gams, L0_gnn_bets), axis=-1)
    x = _layernorm(x + _L1_gnn_ref(x, edge_index, edge_attr_16, L1_gnn_Wf1, L1_gnn_bf1, L1_gnn_Wf2, L1_gnn_bf2, L1_gnn_Wn1, L1_gnn_bn1, L1_gnn_Wn2, L1_gnn_bn2), axis=-1)
    return x

_drawn_inputs = setup_inputs


def setup_inputs(seed=0):
    import zlib

    import numpy as np

    out = dict(_drawn_inputs(seed))
    spreads = {'L0_gnn_sigma1': (1.0, 0.6),
     'L0_gnn_b1': (0.0, 2.0),
     'L0_gnn_gam1': (1.0, 0.2),
     'L0_gnn_bet1': (0.0, 0.8),
     'L0_gnn_sigma2': (1.0, 0.6),
     'L0_gnn_b2': (0.0, 2.0),
     'L0_gnn_gam2': (1.0, 0.2),
     'L0_gnn_bet2': (0.0, 0.1),
     'L0_gnn_sigmas': (1.0, 0.6),
     'L0_gnn_bs': (0.0, 2.0),
     'L0_gnn_gams': (1.0, 0.2),
     'L0_gnn_bets': (0.0, 0.1),
     'L1_gnn_bf1': (0.0, 0.1),
     'L1_gnn_bf2': (0.0, 0.1),
     'L1_gnn_bn1': (0.0, 2.0),
     'L1_gnn_bn2': (0.0, 0.8)}
    factors = {'L0_gnn_gs': 2.684, 'L0_gnn_mus': 5.574}
    for name, (base, spread) in spreads.items():
        noise = np.random.default_rng([zlib.crc32(name.encode()), seed]).standard_normal(out[name].shape)
        drawn = base * np.exp(spread * noise) if base else spread * noise
        out[name] = jnp.asarray(drawn.astype(out[name].dtype))
    for name, factor in factors.items():
        out[name] = (out[name] * factor).astype(out[name].dtype)
    return out
```

```python
from contextlib import ExitStack

import numpy as np
import concourse.bass as bass
from concourse import mybir

FP32 = mybir.dt.float32
BF16 = mybir.dt.bfloat16
I32 = mybir.dt.int32
U32 = mybir.dt.uint32
ALU = mybir.AluOpType
ACT = mybir.ActivationFunctionType
AX = mybir.AxisListType

P = 128
N = 12500
E = 400000
C = 32
KG = 5
D3 = 3
EA = 16
H = 64
NB = -(-N // P)
LAST = N - (NB - 1) * P
NB1 = NB + 1
EP = E // P
T = 4
CH = T * P
TS = 8
CHS = TS * P
TR = 5
BUFS = 4


def most_chunks(ch):
    return -(-(E // ch + NB) // BUFS) * BUFS


NCT = -(-most_chunks(CH) // P) * P
CQ = NCT // P
MIN_TURNS = E // CH // BUFS, E // CHS // BUFS
MAX_TURNS = most_chunks(CH) // BUFS, most_chunks(CHS) // BUFS
NT = MAX_TURNS[0] + 1
NBUFS = 7
PAD = 1 << 20
ZW = (KG + 1) * C + 1
FW = H + 1
BW = H + 2
MW = 96
BN_EPS = 1e-5
LN_EPS = 1e-5
GMM_EPS = 1e-15


def before(i, u, bufs=2):
    return (i, u - 1) if u else (i - 1, bufs - 1)


def turns(engine, n, step, last=None, bufs=2):
    n, final = n if isinstance(n, tuple) else (n, n - 1)
    for u in range(bufs):
        step(0, u)
    with engine.Fori(1, n) as i:
        for u in range(bufs):
            step(i, u)
    if last is not None:
        last(final, bufs - 1)


def started(i):
    return not (isinstance(i, int) and i == 0)


def plain(engine, go):
    engine.sem_inc(go, 1)


def build(nc, x, src, dst, ea16, ea3, w, out):
    ctx = ExitStack()
    with ctx:
        def sb(name, shape, dt=FP32):
            return ctx.enter_context(nc.sbuf_tensor(name, shape, dt))

        def sem(name):
            return ctx.enter_context(nc.semaphore(name))

        s_src = nc.dram_tensor("edges_src", (E + CH,), I32).ap()
        s_dst = nc.dram_tensor("edges_dst", (E + CH,), I32).ap()
        s_ea3 = nc.dram_tensor("edges_ea3", (E + CH, D3), FP32).ap()
        s_ea16 = nc.dram_tensor("edges_ea16", (E + CH, EA), FP32).ap()
        h_dram = nc.dram_tensor("h_rows", (NB * P, C), FP32).ap()
        qp_dram = nc.dram_tensor("qp_rows", (NB * P, 2 * H), FP32).ap()
        bwd_dram = nc.dram_tensor("backward_rows", (E + CHS, BW), FP32).ap()
        tab_i = [nc.dram_tensor(f"chunk_tables_i{k}", (2, NCT), I32).ap() for k in range(2)]
        tab_f = [nc.dram_tensor(f"chunk_tables_f{k}", (1, NCT), FP32).ap() for k in range(2)]

        Z = sb("Z", [P, NB1 * ZW])
        X = sb("X", [P, NB * C])
        YHF = sb("YHF", [P, NB1 * P])
        Y = YHF[:, 0:NB * 2 * C]
        HT = YHF[:, NB * 2 * C:NB * 3 * C]
        F = YHF[0:FW, :]
        RC = sb("RC", [P, NB])
        row_off = [sb(f"row_off{k}", [1, NCT], I32) for k in range(2)]
        row_blk = [sb(f"row_blk{k}", [1, NCT], I32) for k in range(2)]
        base = [sb(f"base{k}", [P, NCT]) for k in range(2)]
        first = [sb(f"first{k}", [P, NB1]) for k in range(2)]
        loops = sb("loops", [P, 8], I32)
        flags = sb("flags", [P, 1], I32)
        col = sb("col", [P, P])
        part = sb("part", [P, 1])
        ident = sb("ident", [P, P])
        ones = sb("ones", [P, P])
        ones_b = sb("ones_b", [P, P], BF16)
        lower_b = sb("lower_b", [P, P], BF16)
        upper_b = sb("upper_b", [P, P], BF16)
        valid = sb("valid", [P, 1])
        thr, thr_h = sb("thr", [P, NT]), sb("thr_h", [P, NT])
        below = [sb(f"below{k}", [P, NT]) for k in range(2)]

        go = sem("waits_met")
        consts = (col, part, ident, ones, ones_b, lower_b, upper_b, valid)
        edges = (s_src, s_dst, s_ea3, s_ea16)
        edge_counts(nc, sem, src, dst, ea3, ea16, edges, Z, Y, consts, thr, thr_h, below[0], flags, x, X, bwd_dram)

        def tables(k, ch, half):
            chunk_tables(nc, k, f"tables{k}", ch, below[k], half, first[k], col, ones, tab_i[k], tab_f[k],
                         row_off[k], row_blk[k], base[k], loops)
        tables(0, CH, False)
        order_edges(nc, go, src, dst, ea3, ea16, edges, flags, first[0], col, ones, ones_b, lower_b, upper_b)
        mu, nis, wt = load_weights(nc, ctx, sb, sem, w)
        by_target = (row_off[0], row_blk[0], base[0], loops)
        gmm_sums(nc, go, "conv1", edges[0:3], x, KG + 1, True, mu, nis, 0, Z, col, *by_target,
                 tally=(Y[:, 0:EP], Y[:, EP:2 * EP], thr_h, below[1]))
        counts(nc, "counts", Z, RC)
        node_products(nc, "out1", [(Z, ZW, (KG + 1) * C, RC), (X, C, C, None)], True,
                      [wt["w1a"], wt["w1b"]], 2 * C, Y, 2 * C, ident)
        batch_norm(nc, "bn1", Y, 2 * C, 0, 2 * C, Z, ones, valid, wt["gam1s"], wt["bet1s"])
        elu_rows(nc, "elu1", Y, 2 * C, HT, valid, Z, h_dram)
        gmm_sums(nc, go, "conv2", edges[0:3], h_dram, KG, False, mu, nis, KG + 1, Z, col, *by_target)
        node_products(nc, "out2", [(Z, ZW, KG * C, RC), (HT, C, C, None)], True,
                      [wt["w2a"], wt["w2b"]], C, Y, 2 * C, ident)
        batch_norm(nc, "bn2", Y, 2 * C, 0, C, Z, ones, valid, wt["gam2"], wt["bet2"])
        add_and_norm(nc, "ln1", Y, X, Z)
        tables(1, CHS, True)
        node_products(nc, "pq", [(X, C, C, None)], False, [wt["wpq"]], 2 * H, Z, 2 * H, ident)
        pq_rows(nc, "pqrows", Z, qp_dram, F)
        flow(nc, go, "flow", s_src, s_dst, s_ea16, qp_dram, bwd_dram, Z, F, wt, ident, col, ones, ones_b,
             lower_b, upper_b, first[1], *by_target)
        backward_sums(nc, go, "bwd", bwd_dram, F, col, row_off[1], row_blk[1], base[1], loops)
        node_mlp(nc, go, "mlp", F, X, wt)
        final_norm(nc, "ln2", X, Z, out)


class Semaphores:

    def __init__(self, nc, own, tag):
        self.nc, self.tag, self.all = nc, tag, []
        own.callback(self.give_back)

    def __call__(self, name):
        self.all.append(self.nc.alloc_semaphore(f"{self.tag}_{name}"))
        return self.all[-1]

    def each(self, name, bufs=2):
        return [self(f"{name}{u}") for u in range(bufs)]

    def give_back(self):
        self.nc.clear_and_free_semaphores(self.all)
        self.nc.all_engine_barrier()


def chained(engine, done):
    count = [0]

    def link(instruction):
        count[0] += 1
        instruction.then_inc(done, 1)
        engine.wait_ge(done, count[0])
    return link


def looped(engine, done, per_turn, bufs=2):
    state = {}

    def begin(i, u):
        assert state.get("n", per_turn) == per_turn
        state.update(at=(i * bufs + u) * per_turn, n=0)

    def link(instruction):
        state["n"] += 1
        assert state["n"] <= per_turn
        instruction.then_inc(done, 1)
        engine.wait_ge(done, state["at"] + state["n"])
    return begin, link


def edge_counts(nc, sem_of, src, dst, ea3, ea16, edges, Z, Y, consts, thr, thr_h, below, flags, x, X, bwd_dram):
    col, part, ident, ones, ones_b, lower_b, upper_b, valid = consts
    s_src, s_dst, s_ea3, s_ea16 = edges
    dst_i = Z[:, 0:EP].bitcast(I32)
    nxt_i = Z[:, EP:2 * EP].bitcast(I32)
    src_i = Z[:, 2 * EP:3 * EP].bitcast(I32)
    dst_f = Z[:, 3 * EP:4 * EP]
    junk, junk_act = Z[:, 4 * EP:5 * EP], Z[:, 5 * EP:6 * EP]
    src_f = Y[:, 0:EP]
    HALF = NB1 // 2
    with ExitStack() as own:
        sem = Semaphores(nc, own, "edges")
        pad_i = own.enter_context(nc.sbuf_tensor("pad_i", [P, T], I32))
        zero_i = own.enter_context(nc.sbuf_tensor("zero_i", [P, T], I32))
        zeros = own.enter_context(nc.sbuf_tensor("zeros", [P, TS, BW], FP32))
        dst_in, nxt_in, src_in, last_set, iotas, vec, order_seen, found, flag_ready, counted, differed, keys_ready = (
            sem(n) for n in ("dst_in", "nxt_in", "src_in", "last_set", "iotas", "vec", "order_seen", "found",
                             "flag_ready", "counted", "differed", "keys_ready"))
        pads, put, copied, x_in = sem("pads"), sem("put"), sem("copied"), sem("x_in")
        viol = own.enter_context(nc.sbuf_tensor("viol", [P, 1], FP32))
        found_p = own.enter_context(nc.psum_tensor("found_p", [P, 512], FP32))
        block = own.enter_context(nc.Block())

        @block.sync
        def _(sp):
            sp.dma_start(dst_i, dst.rearrange("(p t) -> p t", t=EP)).then_inc(dst_in, 16)
            sp.wait_ge(last_set, 1)
            sp.dma_start(nxt_i[0:P - 1, :], dst[1:1 + (P - 1) * EP].rearrange("(p t) -> p t", t=EP)).then_inc(nxt_in, 16)
            sp.dma_start(nxt_i[P - 1:P, 0:EP - 1], dst[1 + (P - 1) * EP:E].rearrange("(p t) -> p t", p=1)).then_inc(nxt_in, 16)
            sp.dma_start(src_i, src.rearrange("(p t) -> p t", t=EP)).then_inc(src_in, 16)
            sp.wait_ge(pads, 5)
            Xv = X[:, :].rearrange("p (b c) -> p b c", c=C)
            sp.dma_start(Xv[:, 0:NB - 1, :], x[0:(NB - 1) * P, :].rearrange("(b p) c -> p b c", p=P)).then_inc(x_in, 16)
            sp.dma_start(Xv[0:LAST, NB - 1, :], x[(NB - 1) * P:N, :]).then_inc(x_in, 16)
            sp.dma_start(s_src[E:E + CH].rearrange("(p t) -> p t", t=T), zero_i[:, :]).then_inc(put, 16)
            sp.dma_start(s_dst[E:E + CH].rearrange("(p t) -> p t", t=T), pad_i[:, :]).then_inc(put, 16)
            flat = zeros[:, :, :].rearrange("p t c -> p (t c)")
            sp.dma_start(s_ea3[E:E + CH, :].rearrange("(p t) c -> p (t c)", t=T), flat[:, 0:T * D3]).then_inc(put, 16)
            sp.dma_start(s_ea16[E:E + CH, :].rearrange("(p t) c -> p (t c)", t=T), flat[:, 0:EA * T]).then_inc(put, 16)
            sp.dma_start(bwd_dram[E:E + CHS, :].rearrange("(p t) c -> p (t c)", t=TS), flat).then_inc(put, 16)
            sp.wait_ge(put, 5 * 16)
            sp.wait_ge(x_in, 2 * 16)
            sp.wait_ge(flag_ready, 1)
            out_of_order = sp.value_load(flags[0:1, 0:1], min_val=0, max_val=E)
            with sp.If(out_of_order == 0):
                rows = P * TR * TR
                for to, of in ((s_src, src), (s_dst, dst)):
                    sp.dma_start(to[0:E].rearrange("(r q) -> r q", r=P), of.rearrange("(r q) -> r q", r=P)).then_inc(copied, 16)
                for to, of in ((s_ea3, ea3), (s_ea16, ea16)):
                    sp.dma_start(to[0:E, :].rearrange("(r q) c -> r (q c)", r=rows), of.rearrange("(r q) c -> r (q c)", r=rows)).then_inc(copied, 16)
                sp.wait_ge(copied, 4 * 16)
            with sp.Else():
                sp.wait_ge(flag_ready, 1)
            sp.wait_ge(flag_ready, 1)

        @block.gpsimd
        def _(pool):
            exact = dict(allow_small_or_imprecise_dtypes=True)
            nc.gpsimd.iota(col[:, :], [[1, P]], base=0, channel_multiplier=0, **exact).then_inc(iotas, 1)
            nc.gpsimd.iota(part[:, :], [[0, 1]], base=0, channel_multiplier=1, **exact).then_inc(iotas, 1)
            nc.gpsimd.iota(thr[:, :], [[P, NT]], base=P, channel_multiplier=0, **exact).then_inc(iotas, 1)
            pool.wait_ge(iotas, 3)

        @block.vector
        def _(dve):
            link = chained(dve, vec)
            nc.vector.memset(nxt_i[:, EP - 1:EP], PAD).then_inc(last_set, 1)
            nc.vector.memset(X[:, (NB - 1) * C:NB * C], 0.0).then_inc(pads, 1)
            nc.vector.memset(pad_i[:, :], PAD).then_inc(pads, 1)
            nc.vector.memset(zero_i[:, :], 0).then_inc(pads, 1)
            nc.vector.memset(zeros[:, :, 0:BW - 1], 0.0).then_inc(pads, 1)
            nc.vector.memset(zeros[:, :, BW - 1:BW], float(PAD)).then_inc(pads, 1)
            link(nc.vector.memset(ones[:, :], 1.0))
            link(nc.vector.memset(ones_b[:, :], 1.0))
            dve.wait_ge(iotas, 3)
            link(nc.vector.tensor_scalar(thr_h[:, :], thr[:, :], -0.5, None, ALU.add))
            link(nc.vector.tensor_scalar(ident[:, :], col[:, :], part[:, 0:1], None, ALU.is_equal))
            link(nc.vector.tensor_scalar(lower_b[:, :], col[:, :], part[:, 0:1], None, ALU.is_gt))
            link(nc.vector.tensor_scalar(upper_b[:, :], col[:, :], part[:, 0:1], None, ALU.is_le))
            link(nc.vector.tensor_scalar(valid[:, :], part[:, :], float(LAST), None, ALU.is_lt))
            dve.wait_ge(dst_in, 16)
            nc.vector.tensor_copy(dst_f, dst_i).then_inc(keys_ready, 1)
            dve.wait_ge(nxt_in, 2 * 16)
            link(nc.vector.tensor_tensor(junk, nxt_i, dst_i, ALU.is_lt))
            nc.vector.tensor_reduce(viol[:, :], junk, AX.X, ALU.add).then_inc(order_seen, 1)
            dve.wait_ge(found, 1)
            nc.vector.tensor_copy(flags[:, :], found_p[:, 0:1]).then_inc(flag_ready, 1)
            dve.wait_ge(src_in, 16)
            link(nc.vector.tensor_copy(src_f, src_i))
            dve.wait_ge(keys_ready, 1)
            with dve.Fori(HALF, NB1) as b:
                nc.vector.tensor_scalar(junk, dst_f, thr[:, bass.ds(b, 1)], None, ALU.is_lt, ALU.add,
                                        accum_out=below[:, bass.ds(b, 1)]).then_inc(counted, 1)
                dve.wait_ge(counted, b - (HALF - 1))
            dve.wait_ge(differed, HALF)
            link(nc.vector.tensor_scalar(below[:, 0:HALF], below[:, 0:HALF], float(EP), 0.5, ALU.add, ALU.mult))

        @block.scalar
        def _(act):
            act.wait_ge(vec, 3)
            act.wait_ge(keys_ready, 1)
            with act.Fori(0, HALF) as b:
                nc.scalar.activation(junk_act, dst_f, ACT.Sign, bias=thr_h[:, bass.ds(b, 1)], scale=-1.0,
                                     accum_out=below[:, bass.ds(b, 1)]).then_inc(differed, 1)
                act.wait_ge(differed, b + 1)

        @block.tensor
        def _(pe):
            pe.wait_ge(vec, 1)
            pe.wait_ge(order_seen, 1)
            nc.tensor.matmul(found_p[:, 0:1], ones[:, :], viol[:, :], start=True, stop=True).then_inc(found, 1)


def chunk_tables(nc, k, tag, ch, below, half, first, col, ones, tab_i, tab_f, row_off, row_blk, base, loops):
    with ExitStack() as own:
        def sb1(name, shape, dt=FP32):
            return own.enter_context(nc.sbuf_tensor(f"{tag}_{name}", shape, dt))
        sem = Semaphores(nc, own, tag)
        tot, num, nch, upto, cfirst, obase, zero = (sb1(n, [P, NB1]) for n in ("tot", "num", "nch", "upto", "cfirst", "obase", "zero"))
        num_i, num_j, turn_i = sb1("num_i", [P, NB1], I32), sb1("num_j", [P, NB1], I32), sb1("turn_i", [P, 1], I32)
        cid, blk, off, blk_n = (sb1(n, [P, CQ]) for n in ("cid", "blk", "off", "blk_n"))
        cmp = sb1("cmp", [P, CQ, NB1])
        blk_i, off_i = sb1("blk_i", [P, CQ], I32), sb1("off_i", [P, CQ], I32)
        total_p = own.enter_context(nc.psum_tensor(f"{tag}_total_p", [P, 512], FP32))
        iotas, halved, totals, vec, tables, stored, reread = (
            sem(n) for n in ("iotas", "halved", "totals", "vec", "tables", "stored", "reread"))
        block = own.enter_context(nc.Block())

        @block.sync
        def _(sp):
            sp.wait_ge(tables, 1)
            sp.dma_start(tab_i[0, :].rearrange("(p q) -> p q", q=CQ), off_i[:, :]).then_inc(stored, 16)
            sp.dma_start(tab_i[1, :].rearrange("(p q) -> p q", q=CQ), blk_i[:, :]).then_inc(stored, 16)
            sp.dma_start(tab_f[0, :].rearrange("(p q) -> p q", q=CQ), blk_n[:, :]).then_inc(stored, 16)
            sp.wait_ge(stored, 3 * 16)
            sp.dma_start(row_off[:, :], tab_i[0:1, :]).then_inc(reread, 16)
            sp.dma_start(row_blk[:, :], tab_i[1:2, :]).then_inc(reread, 16)
            sp.dma_start(base[:, :], tab_f[0:1, :].to_broadcast([P, NCT])).then_inc(reread, 16)
            sp.wait_ge(reread, 3 * 16)

        @block.gpsimd
        def _(pool):
            nc.gpsimd.iota(cid[:, :], [[1, CQ]], base=0, channel_multiplier=CQ,
                           allow_small_or_imprecise_dtypes=True).then_inc(iotas, 1)

        @block.vector
        def _(dve):
            link = chained(dve, vec)
            if half:
                nc.vector.tensor_scalar(below[:, 0:NB1], below[:, 0:NB1], float(EP), 0.5, ALU.add, ALU.mult).then_inc(halved, 1)
            link(nc.vector.memset(zero[:, :], 0.0))
            link(nc.vector.memset(first[:, :], 0.0))
            link(nc.vector.memset(cfirst[:, :], 0.0))
            dve.wait_ge(iotas, 1)
            dve.wait_ge(totals, 1)
            link(nc.vector.tensor_copy(tot[:, :], total_p[:, 0:NB1]))
            link(nc.vector.tensor_copy(first[:, 1:NB1], tot[:, 0:NB]))
            link(nc.vector.tensor_tensor(num[:, :], tot[:, :], first[:, :], ALU.subtract))
            link(nc.vector.tensor_scalar(num_i[:, :], num[:, :], float(ch - 1), None, ALU.add))
            link(nc.vector.tensor_scalar(num_j[:, :], num_i[:, :], ch.bit_length() - 1, None, ALU.arith_shift_right))
            link(nc.vector.tensor_copy(nch[:, :], num_j[:, :]))
            link(nc.vector.tensor_tensor_scan(upto[:, :], nch[:, :], zero[:, :], 0.0, ALU.add, ALU.add))
            link(nc.vector.tensor_scalar(turn_i[:, :], upto[:, NB1 - 1:NB1], float(BUFS - 1), None, ALU.add))
            at = 4 * k
            link(nc.vector.tensor_scalar(loops[:, at:at + 1], turn_i[:, :], BUFS.bit_length() - 1, None, ALU.arith_shift_right))
            link(nc.vector.tensor_scalar(loops[:, at + 1:at + 2], loops[:, at:at + 1], -1.0, None, ALU.add))
            link(nc.vector.tensor_scalar(loops[:, at + 2:at + 3], loops[:, at:at + 1], BUFS / 2, None, ALU.mult))
            link(nc.vector.tensor_scalar(loops[:, at + 3:at + 4], loops[:, at:at + 1], BUFS / 2, -1.0, ALU.mult, ALU.add))
            link(nc.vector.tensor_copy(cfirst[:, 1:NB1], upto[:, 0:NB]))
            link(nc.vector.scalar_tensor_tensor(obase[:, :], cfirst[:, :], -float(ch), first[:, :], ALU.mult, ALU.add))
            link(nc.vector.tensor_tensor(cmp[:, :, 0:NB], cid[:, :].unsqueeze(2).to_broadcast([P, CQ, NB]),
                                         upto[:, 0:NB].unsqueeze(1).to_broadcast([P, CQ, NB]), ALU.is_ge))
            link(nc.vector.tensor_reduce(blk[:, :], cmp[:, :, 0:NB], AX.X, ALU.add))
            link(nc.vector.tensor_scalar(blk_n[:, :], blk[:, :], float(P), None, ALU.mult))
            link(nc.vector.tensor_tensor(cmp[:, :, :], col[:, 0:NB1].unsqueeze(1).to_broadcast([P, CQ, NB1]),
                                         blk[:, :].unsqueeze(2).to_broadcast([P, CQ, NB1]), ALU.is_equal))
            link(nc.vector.tensor_tensor(cmp[:, :, :], cmp[:, :, :],
                                         obase[:, :].unsqueeze(1).to_broadcast([P, CQ, NB1]), ALU.mult))
            link(nc.vector.tensor_reduce(off[:, :], cmp[:, :, :], AX.X, ALU.add))
            link(nc.vector.scalar_tensor_tensor(off[:, :], cid[:, :], float(ch), off[:, :], ALU.mult, ALU.add))
            link(nc.vector.tensor_scalar(off_i[:, :], off[:, :], float(E), None, ALU.min))
            nc.vector.tensor_copy(blk_i[:, :], blk[:, :]).then_inc(tables, 1)

        @block.tensor
        def _(pe):
            if half:
                pe.wait_ge(halved, 1)
            nc.tensor.matmul(total_p[:, 0:NB1], ones[:, :], below[:, 0:NB1], start=True, stop=True).then_inc(totals, 1)


def rank_edges(nc, rank_p, hot_s, tiles, lower_b, ones_b):
    more = dict(start=False, stop=True, skip_group_check=True)
    last = nc.tensor.matmul(rank_p[:, 0:tiles * NB], lower_b[:, :], hot_s, **more)
    for k in range(1, tiles):
        last = nc.tensor.matmul(rank_p[:, k * NB:tiles * NB], ones_b[:, :], hot_s[:, 0:(tiles - k) * NB], **more)
    return last


def complete_ranks(nc, rank_p, hot_s, tiles, upper_b, ones_b):
    more = dict(start=False, stop=True, skip_group_check=True)
    last = nc.tensor.matmul(rank_p[:, 0:tiles * NB], upper_b[:, :], hot_s, **more)
    for k in range(1, tiles):
        last = nc.tensor.matmul(rank_p[:, 0:(tiles - k) * NB], ones_b[:, :], hot_s[:, k * NB:tiles * NB], **more)
    return last


def order_edges(nc, go, src, dst, ea3, ea16, edges, flags, first, col, ones, ones_b, lower_b, upper_b):
    s_src, s_dst, s_ea3, s_ea16 = edges
    STEPS = E // (TR * P)
    with ExitStack() as own:
        def sb1(name, shape, dt=FP32):
            return own.enter_context(nc.sbuf_tensor(f"order_{name}", shape, dt))
        sem = Semaphores(nc, own, "order")
        srci, dsti, blki, idx = (sb1(n, [P, TR], I32) for n in ("srci", "dsti", "blki", "idx"))
        e3, e16 = sb1("e3", [P, TR, D3]), sb1("e16", [P, TR, EA])
        blkf = sb1("blkf", [P, TR])
        begin_row = sb1("begin_row", [1, TR, NB])
        hot_s = sb1("hot_s", [P, TR, NB], BF16)
        sel = sb1("sel", [P, TR, NB])
        rank_p = own.enter_context(nc.psum_tensor("order_rank_p", [P, 512], FP32))
        begins, loaded, vec, hot_ready, ranked, selected, placed, completed = (sem(n) for n in (
            "begins", "loaded", "vec", "hot_ready", "ranked", "selected", "placed", "completed"))
        sent = sem.each("sent", 4)
        block = own.enter_context(nc.Block())

        def if_unordered(engine, body):
            flag = engine.value_load(flags[0:1, 0:1], min_val=0, max_val=E)
            with engine.If(flag > 0):
                body()
            with engine.Else():
                engine.sem_inc(go, 1)
            engine.sem_inc(go, 1)

        def steps(engine, step):
            step(0)
            with engine.Fori(1, STEPS) as i:
                step(i)

        @block.sync
        def _(sp):
            def load(i):
                if started(i):
                    for s in sent:
                        sp.wait_ge(s, i * (TR * 16))
                    plain(sp, go)
                at = bass.ds(i * (TR * P), TR * P)
                sp.dma_start(srci[:, :], src[at].rearrange("(p t) -> p t", t=TR)).then_inc(loaded, 16)
                sp.dma_start(dsti[:, :], dst[at].rearrange("(p t) -> p t", t=TR)).then_inc(loaded, 16)
                sp.dma_start(e3[:, :, :].rearrange("p t c -> p (t c)"), ea3[at, :].rearrange("(p t) c -> p (t c)", t=TR)).then_inc(loaded, 16)
                sp.dma_start(e16[:, :, :].rearrange("p t c -> p (t c)"), ea16[at, :].rearrange("(p t) c -> p (t c)", t=TR)).then_inc(loaded, 16)
            if_unordered(sp, lambda: steps(sp, load))

        @block.vector
        def _(dve):
            def place(i):
                dve.wait_ge(loaded, (i + 1) * 64)
                nc.vector.tensor_scalar(blki[:, :], dsti[:, :], P.bit_length() - 1, None, ALU.arith_shift_right).then_inc(vec, 1)
                dve.wait_ge(vec, 2 * i + 1)
                nc.vector.tensor_copy(blkf[:, :], blki[:, :]).then_inc(vec, 1)
                dve.wait_ge(vec, 2 * i + 2)
                if started(i):
                    dve.wait_ge(completed, i)
                nc.vector.tensor_tensor(hot_s[:, :, :], col[:, 0:NB].unsqueeze(1).to_broadcast([P, TR, NB]),
                                        blkf[:, :].unsqueeze(2).to_broadcast([P, TR, NB]), ALU.is_equal).then_inc(hot_ready, 1)
                dve.wait_ge(ranked, i + 1)
                nc.vector.tensor_tensor(sel[:, :, :], rank_p[:, 0:TR * NB].rearrange("p (t b) -> p t b", b=NB),
                                        hot_s[:, :, :], ALU.mult).then_inc(selected, 1)
                dve.wait_ge(selected, i + 1)
                nc.vector.tensor_reduce(blkf[:, :], sel[:, :, :], AX.X, ALU.add).then_inc(placed, 1)
                dve.wait_ge(placed, 2 * i + 1)
                nc.vector.tensor_copy(idx[:, :], blkf[:, :]).then_inc(placed, 1)

            def body():
                nc.vector.tensor_copy(begin_row[:, :, :], first[0:1, 0:NB].unsqueeze(1).to_broadcast([1, TR, NB])).then_inc(begins, 1)
                steps(dve, place)
            if_unordered(dve, body)

        @block.tensor
        def _(pe):
            def rank(i):
                pe.wait_ge(hot_ready, i + 1)
                hs = hot_s[:, :, :].rearrange("p t b -> p (t b)")
                rank_edges(nc, rank_p, hs, TR, lower_b, ones_b).then_inc(ranked, 1)
                pe.wait_ge(selected, i + 1)
                complete_ranks(nc, rank_p, hs, TR, upper_b, ones_b).then_inc(completed, 1)

            def body():
                pe.wait_ge(begins, 1)
                nc.tensor.matmul(rank_p[:, 0:TR * NB], ones[0:1, :], begin_row[:, :, :].rearrange("p t b -> p (t b)"),
                                 start=True, stop=True, skip_group_check=True)
                steps(pe, rank)
            if_unordered(pe, body)

        @block.gpsimd
        def _(pool):
            def send(i):
                pool.wait_ge(placed, 2 * i + 2)
                plain(pool, go)
                for j in range(TR):
                    for s, to, of in ((sent[0], s_src.unsqueeze(1), srci[:, j:j + 1]), (sent[1], s_dst.unsqueeze(1), dsti[:, j:j + 1]),
                                      (sent[2], s_ea3, e3[:, j, :]), (sent[3], s_ea16, e16[:, j, :])):
                        pool.indirect_dma_start(
                            out=to, out_offset=bass.IndirectOffsetOnAxis(ap=idx[:, j:j + 1].bitcast(U32), axis=0),
                            in_=of, in_offset=None).then_inc(s, 16)

            def body():
                steps(pool, send)
                for s in sent:
                    pool.wait_ge(s, STEPS * TR * 16)
            if_unordered(pool, body)


def load_weights(nc, ctx, sb, sem, w):
    K11 = 2 * KG + 1
    mu = sb("mu", [P, K11, D3])
    nis = sb("nis", [P, K11, D3])
    groups = [("L0_gnn_mu1", "L0_gnn_sigma1", 0, KG), ("L0_gnn_mus", "L0_gnn_sigmas", KG, 1),
              ("L0_gnn_mu2", "L0_gnn_sigma2", KG + 1, KG)]
    wt = {
        "w1a": sb("w1a", [P, MW]), "w1b": sb("w1b", [3 * C + 1, MW]),
        "w2a": sb("w2a", [P, MW]), "w2b": sb("w2b", [2 * C + 1, MW]),
        "gam1s": sb("gam1s", [P, 2 * C]), "bet1s": sb("bet1s", [P, 2 * C]),
        "gam2": sb("gam2", [P, C]), "bet2": sb("bet2", [P, C]),
        "wpq": sb("wpq", [C, 2 * H]), "wc": sb("wc", [P, T, 2 * H]),
        "wf2": sb("wf2", [H + 1, H]), "wn1": sb("wn1", [H, H]), "bn1": sb("bn1", [H, 1]),
        "wn2": sb("wn2", [H + 1, MW]),
    }
    with ExitStack() as own:
        sem = Semaphores(nc, own, "weights")
        cleared, here, vec = sem("cleared"), sem("in"), sem("vec")
        block = own.enter_context(nc.Block())
        loads = []

        def bcast(a):
            return a.unsqueeze(0).to_broadcast([P, a.shape[0]])
        for m, s, k, n in groups:
            loads.append((mu[:, k:k + n, :].rearrange("p k d -> p (k d)"), bcast(w[m].rearrange("k d -> (k d)"))))
            loads.append((nis[:, k:k + n, :].rearrange("p k d -> p (k d)"), bcast(w[s].rearrange("k d -> (k d)"))))
        for k in range(KG):
            for name, g in (("w1", "L0_gnn_g1"), ("w2", "L0_gnn_g2")):
                to = wt[name + "a"][k * C:(k + 1) * C, 0:C] if k < 4 else wt[name + "b"][0:C, 0:C]
                loads.append((to, w[g][:, k * C:(k + 1) * C]))
        loads += [
            (wt["w1b"][C:2 * C, C:2 * C], w["L0_gnn_gs"]),
            (wt["w1b"][2 * C:3 * C, 0:C], w["L0_gnn_root1"]), (wt["w1b"][2 * C:3 * C, C:2 * C], w["L0_gnn_roots"]),
            (wt["w1b"][3 * C:3 * C + 1, 0:C], w["L0_gnn_b1"].unsqueeze(0)),
            (wt["w1b"][3 * C:3 * C + 1, C:2 * C], w["L0_gnn_bs"].unsqueeze(0)),
            (wt["w2b"][C:2 * C, 0:C], w["L0_gnn_root2"]), (wt["w2b"][2 * C:2 * C + 1, 0:C], w["L0_gnn_b2"].unsqueeze(0)),
            (wt["gam1s"][:, 0:C], bcast(w["L0_gnn_gam1"])), (wt["gam1s"][:, C:2 * C], bcast(w["L0_gnn_gams"])),
            (wt["bet1s"][:, 0:C], bcast(w["L0_gnn_bet1"])), (wt["bet1s"][:, C:2 * C], bcast(w["L0_gnn_bets"])),
            (wt["gam2"][:, :], bcast(w["L0_gnn_gam2"])), (wt["bet2"][:, :], bcast(w["L0_gnn_bet2"])),
            (wt["wpq"][:, 0:H], w["L1_gnn_Wf1"][0:C, :]), (wt["wpq"][:, H:2 * H], w["L1_gnn_Wf1"][C:2 * C, :]),
            (wt["wf2"][0:H, :], w["L1_gnn_Wf2"]), (wt["wf2"][H:H + 1, :], w["L1_gnn_bf2"].unsqueeze(0)),
            (wt["wn1"][:, :], w["L1_gnn_Wn1"]), (wt["bn1"][:, :], w["L1_gnn_bn1"].unsqueeze(1)),
            (wt["wn2"][0:H, 0:C], w["L1_gnn_Wn2"]), (wt["wn2"][H:H + 1, 0:C], w["L1_gnn_bn2"].unsqueeze(0)),
        ]
        for j in range(T):
            for half in range(2):
                to = wt["wc"][j * C:j * C + EA, j, half * H:(half + 1) * H]
                loads.append((to, w["L1_gnn_Wf1"][2 * C:2 * C + EA, :]))
                loads.append((wt["wc"][j * C + EA:j * C + EA + 1, j, half * H:(half + 1) * H], w["L1_gnn_bf1"].unsqueeze(0)))

        @block.sync
        def _(sp):
            sp.wait_ge(cleared, 6)
            for to, of in loads:
                sp.dma_start(to, of).then_inc(here, 16)
            sp.wait_ge(here, 16 * len(loads))

        @block.vector
        def _(dve):
            for name in ("w1a", "w1b", "w2a", "w2b", "wn2"):
                nc.vector.memset(wt[name][:, :], 0.0).then_inc(cleared, 1)
            nc.vector.memset(wt["wc"][:, :, :], 0.0).then_inc(cleared, 1)
            link = chained(dve, vec)
            dve.wait_ge(here, 16 * len(loads))
            link(nc.vector.tensor_tensor(nis[:, :, :], nis[:, :, :], nis[:, :, :], ALU.mult))
            link(nc.vector.tensor_scalar(nis[:, :, :], nis[:, :, :], GMM_EPS, None, ALU.add))
            link(nc.vector.reciprocal(nis[:, :, :], nis[:, :, :]))
            link(nc.vector.tensor_scalar(nis[:, :, :], nis[:, :, :], -0.5, None, ALU.mult))
    return mu, nis, wt


def turns_of(engine, loops, k, bufs=BUFS):
    least, most = (n * (BUFS // bufs) for n in (MIN_TURNS[k], MAX_TURNS[k]))
    at = 4 * k + (0 if bufs == BUFS else 2)
    n = engine.snap(engine.value_load(loops[0:1, at:at + 1], min_val=least, max_val=most))
    final = engine.snap(engine.value_load(loops[0:1, at + 1:at + 2], min_val=least - 1, max_val=most - 1))
    return n, final


def gmm_sums(nc, go, tag, edge_rows, table, K, with_count, mu, nis, k0, Z, col, row_off, row_blk, base, loops, tally=None):
    s_src, s_dst, s_ea3 = edge_rows
    W = K * C + (1 if with_count else 0)
    with ExitStack() as own:
        def each(name, shape, dt=FP32):
            return [own.enter_context(nc.sbuf_tensor(f"{tag}_{name}{u}", shape, dt)) for u in range(BUFS)]

        sem = Semaphores(nc, own, tag)


        def sem2(name):
            return sem.each(name, BUFS)
        srci, dsti = each("srci", [P, T], I32), each("dsti", [P, T], I32)
        ea = each("ea", [P, T, D3])
        rows = each("rows", [P, T, C])
        lo = each("lo", [P, T])
        hot = each("hot", [P, T, P])
        dif, sq, sc = each("dif", [P, T, K, D3]), each("sq", [P, T, K, D3]), each("sc", [P, T, K, D3])
        logw, wgt = each("logw", [P, T, K]), each("wgt", [P, T, K])
        wx = each("wx", [P, T, W])
        agg = [own.enter_context(nc.psum_tensor(f"{tag}_agg{u}", [P, 512], FP32)) for u in range(BUFS)]
        loaded, gathered = sem2("loaded"), sem2("gathered")
        logw_ready, w_ready, wx_ready = sem2("logw_ready"), sem2("w_ready"), sem2("wx_ready")
        agg_done, added, vec, cleared = sem2("agg_done"), sem2("added"), sem("vec"), sem("cleared")
        tallied = sem("tallied")
        block = own.enter_context(nc.Block())

        @block.sync
        def _(sp):
            def load(i, u):
                off = sp.value_load(row_off[0:1, bass.ds(BUFS * i + u, 1)], min_val=0, max_val=E)
                if started(i):
                    sp.wait_ge(wx_ready[u], i)
                    plain(sp, go)
                sp.dma_start(srci[u][:, :], s_src[bass.ds(off, CH)].rearrange("(p t) -> p t", t=T)).then_inc(loaded[u], 16)
                sp.dma_start(dsti[u][:, :], s_dst[bass.ds(off, CH)].rearrange("(p t) -> p t", t=T)).then_inc(loaded[u], 16)
                sp.dma_start(ea[u][:, :, :].rearrange("p t d -> p (t d)"),
                             s_ea3[bass.ds(off, CH), :].rearrange("(p t) d -> p (t d)", t=T)).then_inc(loaded[u], 16)
            turns(sp, turns_of(sp, loops, 0), load, bufs=BUFS)

        @block.gpsimd
        def _(pool):
            def gather(i, u):
                pool.wait_ge(loaded[u], (i + 1) * 48)
                plain(pool, go)
                for j in range(T):
                    pool.indirect_dma_start(
                        out=rows[u][:, j, :], out_offset=None, in_=table[:, :],
                        in_offset=bass.IndirectOffsetOnAxis(ap=srci[u][:, j:j + 1].bitcast(U32), axis=0),
                    ).then_inc(gathered[u], 16)
            turns(pool, turns_of(pool, loops, 0), gather, bufs=BUFS)

        @block.vector
        def _(dve):
            begin, link = looped(dve, vec, 4, BUFS)
            link0 = chained(dve, cleared)
            link0(nc.vector.memset(Z[:, :], 0.0))
            if with_count:
                for u in range(BUFS):
                    link0(nc.vector.memset(wx[u][:, :, K * C:W], 1.0))

            def add(i, u):
                b = dve.value_load(row_blk[0:1, bass.ds(BUFS * i + u, 1)], min_val=0, max_val=NB)
                dve.wait_ge(agg_done[u], i + 1)
                if started(i) or u:
                    dve.wait_ge(added[u - 1], before(i, u, BUFS)[0] + 1)
                z = Z[:, bass.ds(b * ZW, W)]
                nc.vector.tensor_tensor(z, z, agg[u][:, 0:W], ALU.add).then_inc(added[u], 1)

            def weigh(i, u):
                begin(i, u)
                dve.wait_ge(loaded[u], (i + 1) * 48)
                link(nc.vector.tensor_scalar(lo[u][:, :], dsti[u][:, :], base[:, bass.ds(BUFS * i + u, 1)], None, ALU.subtract))
                link(nc.vector.tensor_tensor(dif[u][:, :, :, :], ea[u][:, :, :].unsqueeze(2).to_broadcast([P, T, K, D3]),
                                             mu[:, k0:k0 + K, :].unsqueeze(1).to_broadcast([P, T, K, D3]), ALU.subtract))
                link(nc.vector.tensor_tensor(sq[u][:, :, :, :], dif[u][:, :, :, :], dif[u][:, :, :, :], ALU.mult))
                link(nc.vector.tensor_tensor(sc[u][:, :, :, :], sq[u][:, :, :, :],
                                             nis[:, k0:k0 + K, :].unsqueeze(1).to_broadcast([P, T, K, D3]), ALU.mult))
                nc.vector.tensor_reduce(logw[u][:, :, :], sc[u][:, :, :, :], AX.X, ALU.add).then_inc(logw_ready[u], 1)
                if started(i):
                    dve.wait_ge(agg_done[u], i)
                nc.vector.tensor_tensor(hot[u][:, :, :], col[:, :].unsqueeze(1).to_broadcast([P, T, P]),
                                        lo[u][:, :].unsqueeze(2).to_broadcast([P, T, P]), ALU.is_equal)
                if started(i) or u:
                    add(*before(i, u, BUFS))
                dve.wait_ge(gathered[u], (i + 1) * 16 * T)
                dve.wait_ge(w_ready[u], i + 1)
                nc.vector.tensor_tensor(wx[u][:, :, 0:K * C].rearrange("p t (k c) -> p t k c", c=C),
                                        rows[u][:, :, :].unsqueeze(2).to_broadcast([P, T, K, C]),
                                        wgt[u][:, :, :].unsqueeze(3).to_broadcast([P, T, K, C]), ALU.mult).then_inc(wx_ready[u], 1)
            turns(dve, turns_of(dve, loops, 0), weigh, add, bufs=BUFS)

        @block.scalar
        def _(act):
            def exponent(i, u):
                if tally is not None and u == 0:
                    src_f, junk, thr, diff = tally
                    if started(i):
                        act.wait_ge(tallied, i)
                    nc.scalar.activation(junk, src_f, ACT.Sign, bias=thr[:, bass.ds(i, 1)], scale=-1.0,
                                         accum_out=diff[:, bass.ds(i, 1)]).then_inc(tallied, 1)
                act.wait_ge(logw_ready[u], i + 1)
                nc.scalar.activation(wgt[u][:, :, :], logw[u][:, :, :], ACT.Exp).then_inc(w_ready[u], 1)
            turns(act, turns_of(act, loops, 0), exponent, bufs=BUFS)

        @block.tensor
        def _(pe):
            def scatter(i, u):
                pe.wait_ge(wx_ready[u], i + 1)
                if started(i):
                    pe.wait_ge(added[u], i)
                for j in range(T):
                    last = nc.tensor.matmul(agg[u][:, 0:W], hot[u][:, j, :], wx[u][:, j, :], start=(j == 0), stop=(j == T - 1))
                last.then_inc(agg_done[u], 1)
            turns(pe, turns_of(pe, loops, 0), scatter, bufs=BUFS)


def counts(nc, tag, Z, RC):
    with ExitStack() as own:
        sem = Semaphores(nc, own, tag)
        vec = sem("vec")
        block = own.enter_context(nc.Block())

        @block.vector
        def _(dve):
            link = chained(dve, vec)
            cnt = Z[:, 0:NB * ZW].rearrange("p (b w) -> p b w", w=ZW)[:, :, ZW - 1]
            link(nc.vector.tensor_scalar(RC[:, :], cnt, 1.0, None, ALU.max))
            link(nc.vector.reciprocal(RC[:, :], RC[:, :]))


def node_products(nc, tag, parts, with_one, weights, OW, dest, dpitch, ident):
    width = sum(p[2] for p in parts) + int(with_one)
    cuts = [(a, min(a + P, width)) for a in range(0, width, P)]
    OUT = 2 * P
    with ExitStack() as own:
        def each(name, shape, dt=FP32, make=None):
            return [own.enter_context((make or nc.sbuf_tensor)(f"{tag}_{name}{u}", shape, dt)) for u in range(NBUFS)]
        sem = Semaphores(nc, own, tag)
        stage = each("stage", [P, width])
        turned = each("turned", [P, len(cuts), P])
        bank = each("bank", [P, 512], make=nc.psum_tensor)
        staged, transposed, copied, done, saved = (sem.each(s, NBUFS) for s in ("staged", "transposed", "copied", "done", "saved"))
        one_set = sem("one_set")
        block = own.enter_context(nc.Block())
        starts = [sum(p[2] for p in parts[:n]) for n in range(len(parts))]

        @block.gpsimd
        def _(pool):
            def put_second(i, u):
                if started(i):
                    pool.wait_ge(transposed[u], i)
                t, pitch, n, _ = parts[1]
                nc.gpsimd.tensor_copy(stage[u][:, starts[1]:starts[1] + n],
                                      t[:, bass.ds((NBUFS * i + u) * pitch, n)]).then_inc(staged[u], 1)
            if len(parts) > 1:
                turns(pool, NB // NBUFS, put_second, bufs=NBUFS)

        @block.vector
        def _(dve):
            if with_one:
                for u in range(NBUFS):
                    nc.vector.memset(stage[u][:, width - 1:width], 1.0).then_inc(one_set, 1)

            def save(i, u):
                dve.wait_ge(done[u], i + 1)
                nc.vector.tensor_copy(dest[:, bass.ds((NBUFS * i + u) * dpitch, OW)], bank[u][:, OUT:OUT + OW]).then_inc(saved[u], 1)

            def put_first(i, u):
                if started(i):
                    dve.wait_ge(transposed[u], i)
                t, pitch, n, scale = parts[0]
                from_ = t[:, bass.ds((NBUFS * i + u) * pitch, n)]
                if scale is None:
                    nc.vector.tensor_copy(stage[u][:, 0:n], from_).then_inc(staged[u], 1)
                else:
                    nc.vector.tensor_scalar(stage[u][:, 0:n], from_, scale[:, bass.ds(NBUFS * i + u, 1)], None, ALU.mult).then_inc(staged[u], 1)
                if started(i) or u >= 2:
                    save(*earlier(i, u, 2))

            def rest(i, u):
                save(i, u - 1)
                save(i, u)
            turns(dve, NB // NBUFS, put_first, rest, NBUFS)

        @block.scalar
        def _(act):
            def copy(i, u):
                act.wait_ge(transposed[u], i + 1)
                if started(i):
                    act.wait_ge(done[u], i)
                for n, (a, b) in enumerate(cuts):
                    nc.scalar.activation(turned[u][0:b - a, n, :], bank[u][0:b - a, n * P:(n + 1) * P], ACT.Copy).then_inc(copied[u], 1)
            turns(act, NB // NBUFS, copy, bufs=NBUFS)

        @block.tensor
        def _(pe):
            def multiply(i, u):
                pe.wait_ge(copied[u], (i + 1) * len(cuts))
                if started(i):
                    pe.wait_ge(saved[u], i)
                for n, (a, b) in enumerate(cuts):
                    wn = weights[n][0:b - a, :]
                    last = nc.tensor.matmul(bank[u][:, OUT:OUT + wn.shape[1]], turned[u][0:b - a, n, :], wn,
                                            start=(n == 0), stop=(n == len(cuts) - 1))
                last.then_inc(done[u], 1)

            def transpose(i, u):
                pe.wait_ge(staged[u], (i + 1) * len(parts))
                if with_one and not started(i):
                    pe.wait_ge(one_set, NBUFS)
                if started(i):
                    pe.wait_ge(copied[u], i * len(cuts))
                for n, (a, b) in enumerate(cuts):
                    last = nc.tensor.transpose(bank[u][0:b - a, n * P:(n + 1) * P], stage[u][:, a:b], ident[:, :])
                last.then_inc(transposed[u], 1)
                if started(i) or u:
                    multiply(*earlier(i, u, 1))
            turns(pe, NB // NBUFS, transpose, multiply, NBUFS)


def earlier(i, u, n):
    return (i, u - n) if u >= n else (i - 1, u - n + NBUFS)


def batch_norm(nc, tag, Y, pitch, c0, W, tmp, ones, valid, gamma, beta):
    Yv = Y[:, 0:NB * pitch].rearrange("p (b c) -> p b c", c=pitch)[:, :, c0:c0 + W]
    sqv = tmp[:, 0:NB * W].rearrange("p (b c) -> p b c", c=W)
    with ExitStack() as own:
        def one(name, shape=None):
            return own.enter_context(nc.sbuf_tensor(f"{tag}_{name}", shape or [P, W], FP32))

        sem = Semaphores(nc, own, tag)
        part_sum, part_sq, mean, var, sd, amp = (one(n) for n in ("part_sum", "part_sq", "mean", "var", "sd", "amp"))
        total = own.enter_context(nc.psum_tensor(f"{tag}_total", [P, 512], FP32))
        total2 = own.enter_context(nc.psum_tensor(f"{tag}_total2", [P, 512], FP32))
        vec, summed, mean_ready, squares, var_sum, var_ready, rooted = (
            sem(n) for n in ("vec", "summed", "mean_ready", "squares", "var_sum", "var_ready", "rooted"))
        block = own.enter_context(nc.Block())

        def over(a):
            return a[:, 0:W].unsqueeze(1).to_broadcast([P, NB, W])

        @block.vector
        def _(dve):
            link = chained(dve, vec)
            link(nc.vector.tensor_scalar(Yv[:, NB - 1, :], Yv[:, NB - 1, :], valid[:, 0:1], None, ALU.mult))
            nc.vector.tensor_reduce(part_sum[:, :], Yv.rearrange("p b c -> p c b"), AX.X, ALU.add).then_inc(summed, 1)
            dve.wait_ge(mean_ready, 1)
            link(nc.vector.tensor_scalar(mean[:, :], total[:, 0:W], 1.0 / N, None, ALU.mult))
            link(nc.vector.tensor_tensor(Yv, Yv, over(mean), ALU.subtract))
            link(nc.vector.tensor_scalar(Yv[:, NB - 1, :], Yv[:, NB - 1, :], valid[:, 0:1], None, ALU.mult))
            link(nc.vector.tensor_tensor(sqv, Yv, Yv, ALU.mult))
            nc.vector.tensor_reduce(part_sq[:, :], sqv.rearrange("p b c -> p c b"), AX.X, ALU.add).then_inc(squares, 1)
            dve.wait_ge(var_sum, 1)
            nc.vector.tensor_scalar(var[:, :], total2[:, 0:W], 1.0 / N, BN_EPS, ALU.mult, ALU.add).then_inc(var_ready, 1)
            dve.wait_ge(rooted, 1)
            link(nc.vector.reciprocal(amp[:, :], sd[:, :]))
            link(nc.vector.tensor_tensor(amp[:, :], amp[:, :], gamma[:, 0:W], ALU.mult))
            link(nc.vector.tensor_tensor(Yv, Yv, over(amp), ALU.mult))
            link(nc.vector.tensor_tensor(Yv, Yv, over(beta), ALU.add))

        @block.tensor
        def _(pe):
            pe.wait_ge(summed, 1)
            nc.tensor.matmul(total[:, 0:W], ones[:, :], part_sum[:, :], start=True, stop=True).then_inc(mean_ready, 1)
            pe.wait_ge(squares, 1)
            nc.tensor.matmul(total2[:, 0:W], ones[:, :], part_sq[:, :], start=True, stop=True).then_inc(var_sum, 1)

        @block.scalar
        def _(act):
            act.wait_ge(var_ready, 1)
            nc.scalar.activation(sd[:, :], var[:, :], ACT.Sqrt).then_inc(rooted, 1)


def by_block(a, w, pitch=None, n=NB):
    return a[:, 0:n * (pitch or w)].rearrange("p (b c) -> p b c", c=pitch or w)[:, :, 0:w]


def elu_rows(nc, tag, Y, pitch, HT, valid, tmp, h_dram):
    Yv, Hv = by_block(Y, C, pitch), by_block(HT, C)
    low = by_block(tmp, C)
    ex = tmp[:, NB * C:2 * NB * C].rearrange("p (b c) -> p b c", c=C)
    with ExitStack() as own:
        sem = Semaphores(nc, own, tag)
        vec, low_ready, ex_ready, h_ready, stored = (sem(n) for n in ("vec", "low_ready", "ex_ready", "h_ready", "stored"))
        block = own.enter_context(nc.Block())

        @block.vector
        def _(dve):
            link = chained(dve, vec)
            nc.vector.tensor_scalar(low, Yv, 0.0, None, ALU.min).then_inc(low_ready, 1)
            link(nc.vector.tensor_scalar(Hv, Yv, 0.0, -1.0, ALU.max, ALU.add))
            dve.wait_ge(ex_ready, 1)
            link(nc.vector.tensor_tensor(Hv, Hv, ex, ALU.add))
            nc.vector.tensor_scalar(Hv[:, NB - 1, :], Hv[:, NB - 1, :], valid[:, 0:1], None, ALU.mult).then_inc(h_ready, 1)

        @block.scalar
        def _(act):
            act.wait_ge(low_ready, 1)
            nc.scalar.activation(ex, low, ACT.Exp).then_inc(ex_ready, 1)

        @block.sync
        def _(sp):
            sp.wait_ge(h_ready, 1)
            sp.dma_start(h_dram.rearrange("(b p) c -> p b c", p=P), Hv).then_inc(stored, 16)
            sp.wait_ge(stored, 16)


def norm_steps(dve, link, Xv, sqv, stat, var_ready, rooted, sd):
    def over(a):
        return a[:, :].unsqueeze(2).to_broadcast([P, NB, C])
    link(nc_v(dve).tensor_reduce(stat[:, :], Xv, AX.X, ALU.add))
    link(nc_v(dve).tensor_scalar(stat[:, :], stat[:, :], 1.0 / C, None, ALU.mult))
    link(nc_v(dve).tensor_tensor(Xv, Xv, over(stat), ALU.subtract))
    link(nc_v(dve).tensor_tensor(sqv, Xv, Xv, ALU.mult))
    link(nc_v(dve).tensor_reduce(stat[:, :], sqv, AX.X, ALU.add))
    nc_v(dve).tensor_scalar(stat[:, :], stat[:, :], 1.0 / C, LN_EPS, ALU.mult, ALU.add).then_inc(var_ready, 1)
    dve.wait_ge(rooted, 1)
    link(nc_v(dve).reciprocal(stat[:, :], sd[:, :]))
    return nc_v(dve).tensor_tensor(Xv, Xv, over(stat), ALU.mult)


def nc_v(dve):
    return dve


def add_and_norm(nc, tag, Y, X, tmp):
    hv = by_block(Y, C, 2 * C)
    sv = Y[:, 0:NB * 2 * C].rearrange("p (b c) -> p b c", c=2 * C)[:, :, C:2 * C]
    Xv, low = by_block(X, C), by_block(tmp, C)
    ex = tmp[:, NB * C:2 * NB * C].rearrange("p (b c) -> p b c", c=C)
    with ExitStack() as own:
        sem = Semaphores(nc, own, tag)
        stat = own.enter_context(nc.sbuf_tensor(f"{tag}_stat", [P, NB], FP32))
        sd = own.enter_context(nc.sbuf_tensor(f"{tag}_sd", [P, NB], FP32))
        vec, low_ready, ex_ready, var_ready, rooted = (sem(n) for n in ("vec", "low_ready", "ex_ready", "var_ready", "rooted"))
        block = own.enter_context(nc.Block())

        @block.vector
        def _(dve):
            link = chained(dve, vec)
            link(nc.vector.tensor_tensor(hv, hv, sv, ALU.add))
            nc.vector.tensor_scalar(low, hv, 0.0, None, ALU.min).then_inc(low_ready, 1)
            link(nc.vector.tensor_scalar(hv, hv, 0.0, -1.0, ALU.max, ALU.add))
            link(nc.vector.tensor_tensor(Xv, Xv, hv, ALU.add))
            dve.wait_ge(ex_ready, 1)
            link(nc.vector.tensor_tensor(Xv, Xv, ex, ALU.add))
            link(norm_steps(dve, link, Xv, low, stat, var_ready, rooted, sd))

        @block.scalar
        def _(act):
            act.wait_ge(low_ready, 1)
            nc.scalar.activation(ex, low, ACT.Exp).then_inc(ex_ready, 1)
            act.wait_ge(var_ready, 1)
            nc.scalar.activation(sd[:, :], stat[:, :], ACT.Sqrt).then_inc(rooted, 1)


def final_norm(nc, tag, X, tmp, out):
    Xv, sqv = by_block(X, C), by_block(tmp, C)
    with ExitStack() as own:
        sem = Semaphores(nc, own, tag)
        stat = own.enter_context(nc.sbuf_tensor(f"{tag}_stat", [P, NB], FP32))
        sd = own.enter_context(nc.sbuf_tensor(f"{tag}_sd", [P, NB], FP32))
        vec, var_ready, rooted, ready, written = (sem(n) for n in ("vec", "var_ready", "rooted", "ready", "written"))
        block = own.enter_context(nc.Block())

        @block.vector
        def _(dve):
            norm_steps(dve, chained(dve, vec), Xv, sqv, stat, var_ready, rooted, sd).then_inc(ready, 1)

        @block.scalar
        def _(act):
            act.wait_ge(var_ready, 1)
            nc.scalar.activation(sd[:, :], stat[:, :], ACT.Sqrt).then_inc(rooted, 1)

        @block.sync
        def _(sp):
            sp.wait_ge(ready, 1)
            sp.dma_start(out[0:(NB - 1) * P, :].rearrange("(b p) c -> p b c", p=P), Xv[:, 0:NB - 1, :]).then_inc(written, 16)
            sp.dma_start(out[(NB - 1) * P:N, :], Xv[0:LAST, NB - 1, :]).then_inc(written, 16)
            sp.wait_ge(written, 2 * 16)


def pq_rows(nc, tag, PQ, qp_dram, F):
    PQv = by_block(PQ, 2 * H)
    with ExitStack() as own:
        sem = Semaphores(nc, own, tag)
        stored = sem("stored")
        cleared = sem("cleared")
        block = own.enter_context(nc.Block())

        @block.sync
        def _(sp):
            to = qp_dram.rearrange("(b p) c -> p b c", p=P)
            sp.dma_start(to[:, :, 0:H], PQv[:, :, H:2 * H]).then_inc(stored, 16)
            sp.dma_start(to[:, :, H:2 * H], PQv[:, :, 0:H]).then_inc(stored, 16)
            sp.wait_ge(stored, 32)

        @block.vector
        def _(dve):
            nc.vector.memset(F[:, :], 0.0).then_inc(cleared, 1)
            dve.wait_ge(cleared, 1)


def flow(nc, go, tag, s_src, s_dst, s_ea16, qp_dram, bwd_dram, PQ, F, wt, ident, col, ones, ones_b,
         lower_b, upper_b, first, row_off, row_blk, base, loops):
    with ExitStack() as own:
        def two(name, shape, dt=FP32, make=None):
            return [own.enter_context((make or nc.sbuf_tensor)(f"{tag}_{name}{u}", shape, dt)) for u in range(2)]

        sem = Semaphores(nc, own, tag)

        sem2 = sem.each
        srci, dsti, blki = two("srci", [P, T], I32), two("dsti", [P, T], I32), two("blki", [P, T], I32)
        ea = two("ea", [P, T, C])
        qp = two("qp", [P, T, 2 * H])
        lo, m1, m, hm, srcf = (two(n, [P, T]) for n in ("lo", "m1", "m", "hm", "srcf"))
        hot = two("hot", [P, T, P])
        hot_s = two("hot_s", [P, T, NB], BF16)
        sel = two("sel", [P, T, NB])
        pos, miss = two("pos", [P, T]), two("miss", [P, T])
        idx = two("idx", [P, T], I32)
        hot_t = two("hot_t", [P, T, P])
        ea_t = two("ea_t", [P, P])
        fwd = two("fwd", [P, T, FW])
        bwd = two("bwd", [P, T, BW])
        rank_p = own.enter_context(nc.psum_tensor(f"{tag}_rank_p", [P, 512], FP32))
        hot_p = own.enter_context(nc.psum_tensor(f"{tag}_hot_p", [P, 512], FP32))
        ea_p = own.enter_context(nc.psum_tensor(f"{tag}_ea_p", [P, 512], FP32))
        hid_p = two("hid_p", [P, 512], make=nc.psum_tensor)
        sum_p = two("sum_p", [P, 512], make=nc.psum_tensor)
        (loaded, gathered, keys_read, ea_turned, hot_s_ready, hot_ready, hot_turned, turned_out, hid_done,
         relu_done, fwd_done, added, idx_ready, sent, ranked, rank_read) = (sem2(n) for n in (
             "loaded", "gathered", "keys_read", "ea_turned", "hot_s_ready", "hot_ready", "hot_turned", "turned_out",
             "hid_done", "relu_done", "fwd_done", "added", "idx_ready", "sent", "ranked", "rank_read"))
        vec, init = sem("vec"), sem("init")
        begin_row = own.enter_context(nc.sbuf_tensor(f"{tag}_begin_row", [1, T, NB], FP32))
        INIT = 9
        block = own.enter_context(nc.Block())

        @block.sync
        def _(sp):
            sp.wait_ge(init, INIT)

            def load(i, u):
                off = sp.value_load(row_off[0:1, bass.ds(2 * i + u, 1)], min_val=0, max_val=E)
                if started(i):
                    sp.wait_ge(keys_read[u], i)
                    sp.wait_ge(gathered[u], i * 16 * T)
                    sp.wait_ge(ea_turned[u], i)
                    plain(sp, go)
                sp.dma_start(srci[u][:, :], s_src[bass.ds(off, CH)].rearrange("(p t) -> p t", t=T)).then_inc(loaded[u], 16)
                sp.dma_start(dsti[u][:, :], s_dst[bass.ds(off, CH)].rearrange("(p t) -> p t", t=T)).then_inc(loaded[u], 16)
                sp.dma_start(ea[u][:, :, 0:EA], s_ea16[bass.ds(off, CH), :].rearrange("(p t) d -> p t d", t=T)).then_inc(loaded[u], 16)
            turns(sp, turns_of(sp, loops, 0, 2), load)

        @block.gpsimd
        def _(pool):
            def send(i, u):
                pool.wait_ge(relu_done[u], (i + 1) * 3)
                pool.wait_ge(idx_ready[u], i + 1)
                plain(pool, go)
                for j in range(T):
                    pool.indirect_dma_start(
                        out=bwd_dram[:, :], out_offset=bass.IndirectOffsetOnAxis(ap=idx[u][:, j:j + 1].bitcast(U32), axis=0),
                        in_=bwd[u][:, j, :], in_offset=None, bounds_check=E - 1, oob_is_err=False,
                    ).then_inc(sent[u], 16)

            def gather(i, u):
                pool.wait_ge(loaded[u], (i + 1) * 48)
                if started(i):
                    pool.wait_ge(hid_done[u], i)
                plain(pool, go)
                for j in range(T):
                    pool.indirect_dma_start(
                        out=qp[u][:, j, :], out_offset=None, in_=qp_dram[:, :],
                        in_offset=bass.IndirectOffsetOnAxis(ap=srci[u][:, j:j + 1].bitcast(U32), axis=0),
                    ).then_inc(gathered[u], 16)
                if started(i) or u:
                    send(*before(i, u))
            n = turns_of(pool, loops, 0, 2)
            turns(pool, n, gather, send)
            for u in range(2):
                pool.wait_ge(sent[u], n[0] * (16 * T))

        @block.vector
        def _(dve):
            begin, link = looped(dve, vec, 7)
            nc.vector.tensor_copy(begin_row[:, :, :], first[0:1, 0:NB].unsqueeze(1).to_broadcast([1, T, NB])).then_inc(init, 1)
            for u in range(2):
                nc.vector.memset(ea[u][:, :, :], 0.0).then_inc(init, 1)
                dve.wait_ge(init, 4 * u + 2)
                nc.vector.memset(ea[u][:, :, EA:EA + 1], 1.0).then_inc(init, 1)
                nc.vector.memset(bwd[u][:, :, H:H + 1], 1.0).then_inc(init, 1)
                nc.vector.memset(fwd[u][:, :, H:FW], 1.0).then_inc(init, 1)

            def add(i, u):
                b = dve.value_load(row_blk[0:1, bass.ds(2 * i + u, 1)], min_val=0, max_val=NB)
                dve.wait_ge(fwd_done[u], i + 1)
                if started(i) or u:
                    dve.wait_ge(added[1 - u], before(i, u)[0] + 1)
                f = F[:, bass.ds(b * P, P)]
                nc.vector.tensor_tensor(f, f, sum_p[u][0:FW, 0:P], ALU.add).then_inc(added[u], 1)

            def keys(i, u):
                begin(i, u)
                dve.wait_ge(loaded[u], (i + 1) * 48)
                link(nc.vector.tensor_scalar(lo[u][:, :], dsti[u][:, :], base[:, bass.ds(2 * i + u, 1)], None, ALU.subtract))
                link(nc.vector.tensor_scalar(m1[u][:, :], lo[u][:, :], 0.0, None, ALU.is_ge))
                link(nc.vector.scalar_tensor_tensor(m[u][:, :], lo[u][:, :], float(P), m1[u][:, :], ALU.is_lt, ALU.mult))
                link(nc.vector.tensor_scalar(blki[u][:, :], srci[u][:, :], P.bit_length() - 1, None, ALU.arith_shift_right))
                link(nc.vector.scalar_tensor_tensor(hm[u][:, :], blki[u][:, :], 1.0, m[u][:, :], ALU.add, ALU.mult))
                if started(i):
                    dve.wait_ge(relu_done[u], i * 3)
                nc.vector.tensor_copy(srcf[u][:, :], srci[u][:, :]).then_inc(keys_read[u], 1)
                if started(i):
                    dve.wait_ge(ranked[u], 2 * i)
                nc.vector.tensor_tensor(hot_s[u][:, :, :], col[:, 1:NB + 1].unsqueeze(1).to_broadcast([P, T, NB]),
                                        hm[u][:, :].unsqueeze(2).to_broadcast([P, T, NB]), ALU.is_equal).then_inc(hot_s_ready[u], 1)
                if started(i):
                    dve.wait_ge(fwd_done[u], i)
                nc.vector.tensor_tensor(hot[u][:, :, :], col[:, :].unsqueeze(1).to_broadcast([P, T, P]),
                                        lo[u][:, :].unsqueeze(2).to_broadcast([P, T, P]), ALU.is_equal).then_inc(hot_ready[u], 1)
                dve.wait_ge(ranked[u], 2 * i + 1)
                nc.vector.tensor_tensor(sel[u][:, :, :], rank_p[:, 0:T * NB].rearrange("p (t b) -> p t b", b=NB),
                                        hot_s[u][:, :, :], ALU.mult).then_inc(rank_read[u], 1)
                dve.wait_ge(rank_read[u], i + 1)
                link(nc.vector.tensor_reduce(pos[u][:, :], sel[u][:, :, :], AX.X, ALU.add))
                link(nc.vector.tensor_scalar(miss[u][:, :], m[u][:, :], -float(PAD), float(PAD), ALU.mult, ALU.add))
                if started(i):
                    dve.wait_ge(sent[u], i * 16 * T)
                nc.vector.tensor_tensor(idx[u][:, :], pos[u][:, :], miss[u][:, :], ALU.add).then_inc(idx_ready[u], 1)
                if started(i) or u:
                    add(*before(i, u))
            turns(dve, turns_of(dve, loops, 0, 2), keys, add)

        @block.scalar
        def _(act):
            act.wait_ge(init, INIT)

            def relus(i, u):
                act.wait_ge(hid_done[u], i + 1)
                if started(i):
                    act.wait_ge(fwd_done[u], i)
                    act.wait_ge(sent[u], i * 16 * T)
                hid = hid_p[u][:, :].rearrange("p (t h) -> p t h", h=2 * H)
                nc.scalar.activation(fwd[u][:, :, 0:H], hid[:, :, 0:H], ACT.Relu).then_inc(relu_done[u], 1)
                nc.scalar.activation(bwd[u][:, :, 0:H], hid[:, :, H:2 * H], ACT.Relu).then_inc(relu_done[u], 1)
                act.wait_ge(keys_read[u], i + 1)
                nc.scalar.activation(bwd[u][:, :, H + 1], srcf[u][:, :], ACT.Copy).then_inc(relu_done[u], 1)

            def turned(i, u):
                act.wait_ge(hot_turned[u], i + 1)
                if started(i):
                    act.wait_ge(hid_done[u], i)
                nc.scalar.activation(hot_t[u][:, :, :].rearrange("p t e -> p (t e)"), hot_p[:, :], ACT.Copy).then_inc(turned_out[u], 1)
                act.wait_ge(ea_turned[u], i + 1)
                nc.scalar.activation(ea_t[u][:, :], ea_p[:, 0:P], ACT.Copy).then_inc(turned_out[u], 1)
                if started(i) or u:
                    relus(*before(i, u))
            turns(act, turns_of(act, loops, 0, 2), turned, relus)

        @block.tensor
        def _(pe):
            pe.wait_ge(init, INIT)
            nc.tensor.matmul(rank_p[:, 0:T * NB], ones[0:1, :], begin_row[:, :, :].rearrange("p t b -> p (t b)"),
                             start=True, stop=True, skip_group_check=True)

            def rank(i, u):
                pe.wait_ge(hot_s_ready[u], i + 1)
                hs = hot_s[u][:, :, :].rearrange("p t b -> p (t b)")
                rank_edges(nc, rank_p, hs, T, lower_b, ones_b).then_inc(ranked[u], 1)

            def complete(i, u):
                pe.wait_ge(rank_read[u], i + 1)
                hs = hot_s[u][:, :, :].rearrange("p t b -> p (t b)")
                complete_ranks(nc, rank_p, hs, T, upper_b, ones_b).then_inc(ranked[u], 1)

            def forward(i, u):
                pe.wait_ge(relu_done[u], i * 3 + 1)
                if started(i):
                    pe.wait_ge(added[u], i)
                for j in range(T):
                    last = nc.tensor.matmul(sum_p[u][0:FW, 0:P], fwd[u][:, j, :], hot[u][:, j, :], start=(j == 0), stop=(j == T - 1))
                last.then_inc(fwd_done[u], 1)

            def hidden(i, u):
                b = pe.value_load(row_blk[0:1, bass.ds(2 * i + u, 1)], min_val=0, max_val=NB)
                b = pe.snap(b)
                rank(i, u)
                pe.wait_ge(hot_ready[u], i + 1)
                if started(i) or u:
                    pe.wait_ge(turned_out[1 - u], 2 * before(i, u)[0] + 2)
                for j in range(T):
                    last = nc.tensor.transpose(hot_p[:, j * P:(j + 1) * P], hot[u][:, j, :], ident[:, :])
                last.then_inc(hot_turned[u], 1)
                pe.wait_ge(loaded[u], (i + 1) * 48)
                nc.tensor.transpose(ea_p[:, 0:P], ea[u][:, :, :].rearrange("p t c -> p (t c)"), ident[:, :]).then_inc(ea_turned[u], 1)
                if started(i) or u:
                    forward(*before(i, u))
                complete(i, u)
                pe.wait_ge(turned_out[u], 2 * i + 2)
                if started(i):
                    pe.wait_ge(relu_done[u], i * 3)
                nc.tensor.matmul(hid_p[u][:, :], ea_t[u][:, :], wt["wc"][:, :, :].rearrange("p t h -> p (t h)"), start=True, stop=False)
                for j in range(T):
                    nc.tensor.matmul(hid_p[u][:, j * 2 * H:(j + 1) * 2 * H], hot_t[u][:, j, :],
                                     PQ[:, bass.ds(b * 2 * H, 2 * H)], start=False, stop=False, skip_group_check=True)
                pe.wait_ge(gathered[u], (i + 1) * 16 * T)
                nc.tensor.matmul(hid_p[u][:, :], ident[:, :], qp[u][:, :, :].rearrange("p t h -> p (t h)"),
                                 start=False, stop=True).then_inc(hid_done[u], 1)
            turns(pe, turns_of(pe, loops, 0, 2), hidden, forward)


def backward_sums(nc, go, tag, bwd_dram, F, col, row_off, row_blk, base, loops):
    with ExitStack() as own:
        def each(name, shape, dt=FP32, make=None):
            return [own.enter_context((make or nc.sbuf_tensor)(f"{tag}_{name}{u}", shape, dt)) for u in range(BUFS)]

        sem = Semaphores(nc, own, tag)

        def sem2(name):
            return sem.each(name, BUFS)
        rows = each("rows", [P, TS, BW])
        lo = each("lo", [P, TS])
        hot = each("hot", [P, TS, P])
        sum_p = each("sum_p", [P, 512], make=nc.psum_tensor)
        loaded, lo_ready, hot_ready, sum_done, added = (sem2(n) for n in ("loaded", "lo_ready", "hot_ready", "sum_done", "added"))
        block = own.enter_context(nc.Block())

        @block.sync
        def _(sp):
            def load(i, u):
                off = sp.value_load(row_off[0:1, bass.ds(BUFS * i + u, 1)], min_val=0, max_val=E)
                if started(i):
                    sp.wait_ge(sum_done[u], i)
                    plain(sp, go)
                sp.dma_start(rows[u][:, :, :].rearrange("p t w -> p (t w)"),
                             bwd_dram[bass.ds(off, CHS), :].rearrange("(p t) w -> p (t w)", t=TS)).then_inc(loaded[u], 16)
            turns(sp, turns_of(sp, loops, 1), load, bufs=BUFS)

        @block.vector
        def _(dve):
            def add(i, u):
                b = dve.value_load(row_blk[0:1, bass.ds(BUFS * i + u, 1)], min_val=0, max_val=NB)
                dve.wait_ge(sum_done[u], i + 1)
                if started(i) or u:
                    dve.wait_ge(added[u - 1], before(i, u, BUFS)[0] + 1)
                f = F[:, bass.ds(b * P, P)]
                nc.vector.tensor_tensor(f, f, sum_p[u][0:FW, 0:P], ALU.add).then_inc(added[u], 1)

            def one_hot(i, u):
                dve.wait_ge(loaded[u], (i + 1) * 16)
                nc.vector.tensor_scalar(lo[u][:, :], rows[u][:, :, BW - 1], base[:, bass.ds(BUFS * i + u, 1)], None, ALU.subtract).then_inc(lo_ready[u], 1)
                dve.wait_ge(lo_ready[u], i + 1)
                if started(i):
                    dve.wait_ge(sum_done[u], i)
                nc.vector.tensor_tensor(hot[u][:, :, :], col[:, :].unsqueeze(1).to_broadcast([P, TS, P]),
                                        lo[u][:, :].unsqueeze(2).to_broadcast([P, TS, P]), ALU.is_equal).then_inc(hot_ready[u], 1)
                if started(i) or u:
                    add(*before(i, u, BUFS))
            turns(dve, turns_of(dve, loops, 1), one_hot, add, bufs=BUFS)

        @block.tensor
        def _(pe):
            def sums(i, u):
                pe.wait_ge(hot_ready[u], i + 1)
                if started(i):
                    pe.wait_ge(added[u], i)
                for j in range(TS):
                    last = nc.tensor.matmul(sum_p[u][0:FW, 0:P], rows[u][:, j, 0:FW], hot[u][:, j, :], start=(j == 0), stop=(j == TS - 1))
                last.then_inc(sum_done[u], 1)
            turns(pe, turns_of(pe, loops, 1), sums, bufs=BUFS)


def node_mlp(nc, go, tag, F, X, wt):
    G = 4
    FULL = NB // (2 * G)
    SHORT = NB - FULL * 2 * G
    assert 0 < SHORT < G
    with ExitStack() as own:
        def two(name, shape, dt=FP32, make=None):
            return [own.enter_context((make or nc.sbuf_tensor)(f"{tag}_{name}{u}", shape, dt)) for u in range(2)]
        sem = Semaphores(nc, own, tag)
        flow_s, hid = two("flow_s", [H, G * P]), two("hid", [H + 1, G * P])
        flow_p, hid_p, out_p = (two(n, [P, 512], make=nc.psum_tensor) for n in ("flow_p", "hid_p", "out_p"))
        flow_done, flow_ready, hid_done, hid_ready, out_done, added = (sem.each(n) for n in (
            "flow_done", "flow_ready", "hid_done", "hid_ready", "out_done", "added"))
        one_set = sem("one_set")
        block = own.enter_context(nc.Block())

        def groups(engine, step, last=None):
            turns(engine, FULL, lambda i, u: step(i, u, G))
            step(FULL, 0, SHORT)
            if last is not None:
                last(FULL, 0, SHORT)

        @block.vector
        def _(dve):
            for u in range(2):
                nc.vector.memset(hid[u][H:H + 1, :], 1.0).then_inc(one_set, 1)

            def add(i, u, g):
                dve.wait_ge(out_done[u], i + 1)
                xb = X[:, bass.ds((2 * i + u) * (G * C), g * C)]
                nc.vector.tensor_tensor(xb.rearrange("p (g c) -> p g c", c=C), xb.rearrange("p (g c) -> p g c", c=C),
                                        out_p[u][:, 0:g * P].rearrange("p (g c) -> p g c", c=P)[:, :, 0:C], ALU.add).then_inc(added[u], 1)
            groups(dve, add)

        @block.tensor
        def _(pe):
            pe.wait_ge(one_set, 2)

            def rest(i, u, g):
                pe.wait_ge(flow_ready[u], i + 1)
                plain(pe, go)
                nc.tensor.matmul(hid_p[u][0:H, 0:g * P], wt["wn1"][:, :], flow_s[u][:, 0:g * P], start=True, stop=True).then_inc(hid_done[u], 1)
                pe.wait_ge(hid_ready[u], i + 1)
                if started(i):
                    pe.wait_ge(added[u], i)
                for n in range(g):
                    last = nc.tensor.matmul(out_p[u][:, n * P:n * P + MW], hid[u][:, n * P:(n + 1) * P], wt["wn2"][:, :], start=True, stop=True)
                last.then_inc(out_done[u], 1)

            def sums(i, u, g):
                if started(i):
                    pe.wait_ge(flow_ready[u], i)
                nc.tensor.matmul(flow_p[u][0:H, 0:g * P], wt["wf2"][:, :], F[:, bass.ds((2 * i + u) * (G * P), g * P)],
                                 start=True, stop=True).then_inc(flow_done[u], 1)
                if started(i) or u:
                    rest(*before(i, u), G)
            groups(pe, sums, rest)

        @block.scalar
        def _(act):
            def relu(i, u, g):
                act.wait_ge(hid_done[u], i + 1)
                if started(i):
                    act.wait_ge(out_done[u], i)
                nc.scalar.activation(hid[u][0:H, 0:g * P], hid_p[u][0:H, 0:g * P], ACT.Relu, bias=wt["bn1"][:, 0:1]).then_inc(hid_ready[u], 1)

            def copy(i, u, g):
                act.wait_ge(flow_done[u], i + 1)
                if started(i):
                    act.wait_ge(hid_done[u], i)
                nc.scalar.activation(flow_s[u][:, 0:g * P], flow_p[u][0:H, 0:g * P], ACT.Copy).then_inc(flow_ready[u], 1)
                if started(i) or u:
                    relu(*before(i, u), G)
            groups(act, copy, relu)


WEIGHTS = ["L0_gnn_" + n for n in ("g1", "mu1", "sigma1", "root1", "b1", "gam1", "bet1", "g2", "mu2", "sigma2", "root2",
                                   "b2", "gam2", "bet2", "gs", "mus", "sigmas", "roots", "bs", "gams", "bets")]
WEIGHTS += ["L1_gnn_" + n for n in ("Wf1", "bf1", "Wf2", "bf2", "Wn1", "bn1", "Wn2", "bn2")]


def kernel(**inputs):
    import concourse.bacc as bacc
    from concourse.bass_utils import run_bass_kernel_spmd

    nc = bacc.Bacc("TRN2", target_bir_lowering=False, num_devices=1)
    arrays, aps = {}, {}
    for name in ["x", "src", "dst", "edge_attr_16", "edge_attr_3"] + WEIGHTS:
        a = np.ascontiguousarray(inputs[name])
        arrays[f"in_{name}"] = a
        aps[name] = nc.dram_tensor(f"in_{name}", a.shape, mybir.dt.from_np(a.dtype), kind="ExternalInput").ap()
    out = nc.dram_tensor("out_x", (N, C), FP32, kind="ExternalOutput").ap()
    build(nc, aps["x"], aps["src"], aps["dst"], aps["edge_attr_16"], aps["edge_attr_3"],
          {n: aps[n] for n in WEIGHTS}, out)
    r = run_bass_kernel_spmd(nc, [arrays], core_ids=[0])
    return r.results[0]["out_x"]
```

```python
from contextlib import ExitStack

import numpy as np
import concourse.bass as bass
from concourse import mybir

FP32 = mybir.dt.float32
BF16 = mybir.dt.bfloat16
I32 = mybir.dt.int32
U32 = mybir.dt.uint32
ALU = mybir.AluOpType
ACT = mybir.ActivationFunctionType
AX = mybir.AxisListType

P = 128
N = 12500
E = 400000
C = 32
KG = 5
D3 = 3
EA = 16
H = 64
NB = -(-N // P)
LAST = N - (NB - 1) * P
NB1 = NB + 1
EP = E // P
T = 4
CH = T * P
TS = 8
CHS = TS * P
TR = 5
BUFS = 4


def most_chunks(ch):
    return -(-(E // ch + NB) // BUFS) * BUFS


def table_chunks(ch):
    return -(-most_chunks(ch) // P) * P


SEGS = -(-E // CH)
HW = P // 2
WINDOWS = -(-N // HW)
MIN_TURNS = E // CH // BUFS, E // CHS // BUFS
MAX_TURNS = most_chunks(CH) // BUFS, most_chunks(CHS) // BUFS
NT = MAX_TURNS[0] + 1
NBUFS = 7
PAD = 1 << 20
ZW = (KG + 1) * C + 1
FW = H + 1
BW = H + 2
LONG_ROWS = P * TR * TR
MW = 96
BN_EPS = 1e-5
LN_EPS = 1e-5
GMM_EPS = 1e-15
GAUSSIANS = 6


def before(i, u, bufs=2):
    return (i, u - 1) if u else (i - 1, bufs - 1)


def earlier(i, u, n, bufs=NBUFS):
    return (i, u - n) if u >= n else (i - 1, u - n + bufs)


def turns(engine, n, step, last=None, bufs=2):
    n, final = n if isinstance(n, tuple) else (n, n - 1)
    for u in range(bufs):
        step(0, u)
    with engine.Fori(1, n) as i:
        for u in range(bufs):
            step(i, u)
    if last is not None:
        last(final, bufs - 1)


def started(i):
    return not (isinstance(i, int) and i == 0)


def plain(engine, go):
    engine.sem_inc(go, 1)


def build(nc, x, src, dst, ea16, ea3, w, out):
    ctx = ExitStack()
    with ctx:
        def sb(name, shape, dt=FP32):
            return ctx.enter_context(nc.sbuf_tensor(name, shape, dt))

        def sem(name):
            return ctx.enter_context(nc.semaphore(name))

        s_src = nc.dram_tensor("edges_src", (E + CH,), I32).ap()
        s_dst = nc.dram_tensor("edges_dst", (E + CH,), I32).ap()
        s_ea3 = nc.dram_tensor("edges_ea3", (E + CH, D3), FP32).ap()
        s_ea16 = nc.dram_tensor("edges_ea16", (E + CH, EA), FP32).ap()
        h_dram = nc.dram_tensor("h_rows", (NB * P, C), FP32).ap()
        qp_dram = nc.dram_tensor("qp_rows", (NB * P, 2 * H), FP32).ap()
        bwd_dram = nc.dram_tensor("backward_rows", (E + CHS, BW), FP32).ap()
        NCT, NCS = table_chunks(CH), table_chunks(CHS)
        tab_i = [nc.dram_tensor(f"chunk_tables_i{k}", (r, n), I32).ap() for k, r, n in ((0, 4, NCT), (1, 2, NCS))]
        tab_f = [nc.dram_tensor(f"chunk_tables_f{k}", (1, n), FP32).ap() for k, n in ((0, NCT), (1, NCS))]

        Z = sb("Z", [P, NB1 * ZW])
        X = sb("X", [P, NB * C])
        YHF = sb("YHF", [P, NB1 * P])
        Y = YHF[:, 0:NB * 2 * C]
        HT = YHF[:, NB * 2 * C:NB * 3 * C]
        F = YHF[0:FW, :]
        RC = sb("RC", [P, NB])
        row_off, row_lower, row_upper, row_shift = (sb(n, [1, NCT], I32) for n in ("row_off", "row_lower", "row_upper", "row_shift"))
        less_first = sb("less_first", [P, NCT])
        off_s, blk_s, less_first_s = sb("off_s", [1, NCS], I32), sb("blk_s", [1, NCS], I32), sb("less_first_s", [P, NCS])
        first = [sb(f"first{k}", [P, NB1]) for k in range(2)]
        loops = sb("loops", [P, 8], I32)
        flags = sb("flags", [P, 1], I32)
        col = sb("col", [P, P])
        col2 = sb("col2", [P, 2 * P])
        part = sb("part", [P, 1])
        ident = sb("ident", [P, P])
        ones = sb("ones", [P, P])
        ones_b = sb("ones_b", [P, P], BF16)
        lower_b = sb("lower_b", [P, P], BF16)
        upper_b = sb("upper_b", [P, P], BF16)
        valid = sb("valid", [P, 1])
        thr, thr_h = sb("thr", [P, NT]), sb("thr_h", [P, NT])
        below = [sb(f"below{k}", [P, NT]) for k in range(2)]

        go = sem("waits_met")
        ea16_copied = sem("ea16_copied")
        weights_in = sem("weights_in")
        consts = (col, col2, part, ident, ones, ones_b, lower_b, upper_b, valid)
        edges = (s_src, s_dst, s_ea3, s_ea16)
        mu, nis, wt, clear, loads = weight_tiles(sb, w)
        edge_order(nc, nis, clear, loads, weights_in, src, dst, ea3, ea16, edges, Z, Y, consts, thr, thr_h, flags, x, X, bwd_dram)
        order_edges(nc, go, src, dst, ea3, ea16, edges, flags, Z, below[0], thr, thr_h, first[0], col, ones, ones_b,
                    lower_b, upper_b)
        window_tables(nc, "windows", s_dst, flags, ones, Z, tab_i[0], tab_f[0],
                      (row_off, row_lower, row_upper, row_shift), less_first, loops)
        by_target = (row_off, row_lower, row_upper, row_shift, less_first, loops)
        gmm_sums(nc, go, "conv1", edges[0:3], x, KG + 1, True, mu, nis, 0, Z, col2, *by_target,
                 tally=(Y[:, 0:EP], Y[:, EP:2 * EP], thr_h, below[1]))
        counts(nc, "counts", Z, RC, weights_in, len(loads) - GAUSSIANS, ea16, s_ea16, flags, ea16_copied)
        node_products(nc, "out1", [(Z, ZW, (KG + 1) * C, RC), (X, C, C, None)], True,
                      [wt["w1a"], wt["w1b"]], 2 * C, Y, 2 * C, ident)
        batch_norm(nc, "bn1", Y, 2 * C, 0, 2 * C, Z, ones, valid, wt["gam1s"], wt["bet1s"])
        elu_rows(nc, "elu1", Y, 2 * C, HT, valid, Z, h_dram)
        gmm_sums(nc, go, "conv2", edges[0:3], h_dram, KG, False, mu, nis, KG + 1, Z, col2, *by_target)
        node_products(nc, "out2", [(Z, ZW, KG * C, RC), (HT, C, C, None)], True,
                      [wt["w2a"], wt["w2b"]], C, Y, 2 * C, ident)
        batch_norm(nc, "bn2", Y, 2 * C, 0, C, Z, ones, valid, wt["gam2"], wt["bet2"])
        add_and_norm(nc, "ln1", Y, X, Z)
        block_tables(nc, "blocks", below[1], first[1], col, ones, tab_i[1], tab_f[1], off_s, blk_s, less_first_s, loops)
        node_products(nc, "pq", [(X, C, C, None)], False, [wt["wpq"]], 2 * H, Z, 2 * H, ident)
        pq_rows(nc, "pqrows", Z, qp_dram, F)
        flow(nc, go, "flow", s_src, s_dst, s_ea16, qp_dram, bwd_dram, Z, F, wt, ident, col, col2, ones, ones_b,
             lower_b, upper_b, first[1], ea16_copied, *by_target)
        backward_sums(nc, go, "bwd", bwd_dram, F, col, off_s, blk_s, less_first_s, loops)
        node_mlp(nc, go, "mlp", F, X, wt)
        final_norm(nc, "ln2", X, Z, out)


class Semaphores:

    def __init__(self, nc, own, tag):
        self.nc, self.tag, self.all = nc, tag, []
        own.callback(self.give_back)

    def __call__(self, name):
        self.all.append(self.nc.alloc_semaphore(f"{self.tag}_{name}"))
        return self.all[-1]

    def each(self, name, bufs=2):
        return [self(f"{name}{u}") for u in range(bufs)]

    def give_back(self):
        self.nc.clear_and_free_semaphores(self.all)
        self.nc.all_engine_barrier()


def chained(engine, done):
    count = [0]

    def link(instruction):
        count[0] += 1
        instruction.then_inc(done, 1)
        engine.wait_ge(done, count[0])
    return link


def looped(engine, done, per_turn, bufs=2):
    state = {}

    def begin(i, u):
        assert state.get("n", per_turn) == per_turn
        state.update(at=(i * bufs + u) * per_turn, n=0)

    def link(instruction):
        state["n"] += 1
        assert state["n"] <= per_turn
        instruction.then_inc(done, 1)
        engine.wait_ge(done, state["at"] + state["n"])
    return begin, link


def edge_order(nc, nis, clear, loads, weights_in, src, dst, ea3, ea16, edges, Z, Y, consts, thr, thr_h, flags, x, X, bwd_dram):
    col, col2, part, ident, ones, ones_b, lower_b, upper_b, valid = consts
    s_src, s_dst, s_ea3, s_ea16 = edges
    dst_i = Z[:, 0:EP].bitcast(I32)
    nxt_i = Z[:, EP:2 * EP].bitcast(I32)
    src_i = Z[:, 2 * EP:3 * EP].bitcast(I32)
    dst_f = Z[:, 3 * EP:4 * EP]
    junk = Z[:, 4 * EP:5 * EP]
    src_f = Y[:, 0:EP]
    with ExitStack() as own:
        sem = Semaphores(nc, own, "edges")
        pad_i = own.enter_context(nc.sbuf_tensor("pad_i", [P, T], I32))
        zero_i = own.enter_context(nc.sbuf_tensor("zero_i", [P, T], I32))
        zeros = own.enter_context(nc.sbuf_tensor("zeros", [P, TS, BW], FP32))
        dst_in, nxt_in, src_in, last_set, iotas, vec, order_seen, found, flag_ready = (
            sem(n) for n in ("dst_in", "nxt_in", "src_in", "last_set", "iotas", "vec", "order_seen", "found",
                             "flag_ready"))
        pads, put, copied, x_in = sem("pads"), sem("put"), sem("copied"), sem("x_in")
        cleared, gaussians_in = sem("cleared"), sem("gaussians_in")
        gaussians, rest = loads[:GAUSSIANS], loads[GAUSSIANS:]
        viol = own.enter_context(nc.sbuf_tensor("viol", [P, 1], FP32))
        found_p = own.enter_context(nc.psum_tensor("found_p", [P, 512], FP32))
        block = own.enter_context(nc.Block())

        @block.sync
        def _(sp):
            sp.dma_start(dst_i, dst.rearrange("(p t) -> p t", t=EP)).then_inc(dst_in, 16)
            sp.wait_ge(last_set, 1)
            sp.dma_start(nxt_i[0:P - 1, :], dst[1:1 + (P - 1) * EP].rearrange("(p t) -> p t", t=EP)).then_inc(nxt_in, 16)
            sp.dma_start(nxt_i[P - 1:P, 0:EP - 1], dst[1 + (P - 1) * EP:E].rearrange("(p t) -> p t", p=1)).then_inc(nxt_in, 16)
            sp.dma_start(src_i, src.rearrange("(p t) -> p t", t=EP)).then_inc(src_in, 16)
            sp.wait_ge(pads, 5)
            Xv = X[:, :].rearrange("p (b c) -> p b c", c=C)
            sp.dma_start(Xv[:, 0:NB - 1, :], x[0:(NB - 1) * P, :].rearrange("(b p) c -> p b c", p=P)).then_inc(x_in, 16)
            sp.dma_start(Xv[0:LAST, NB - 1, :], x[(NB - 1) * P:N, :]).then_inc(x_in, 16)
            sp.dma_start(s_src[E:E + CH].rearrange("(p t) -> p t", t=T), zero_i[:, :]).then_inc(put, 16)
            sp.dma_start(s_dst[E:E + CH].rearrange("(p t) -> p t", t=T), pad_i[:, :]).then_inc(put, 16)
            flat = zeros[:, :, :].rearrange("p t c -> p (t c)")
            sp.dma_start(s_ea3[E:E + CH, :].rearrange("(p t) c -> p (t c)", t=T), flat[:, 0:T * D3]).then_inc(put, 16)
            sp.dma_start(s_ea16[E:E + CH, :].rearrange("(p t) c -> p (t c)", t=T), flat[:, 0:EA * T]).then_inc(put, 16)
            sp.dma_start(bwd_dram[E:E + CHS, :].rearrange("(p t) c -> p (t c)", t=TS), flat).then_inc(put, 16)
            for to, of in ((s_dst, dst), (s_src, src)):
                sp.dma_start(to[0:E].rearrange("(r q) -> r q", r=P), of.rearrange("(r q) -> r q", r=P)).then_inc(copied, 16)
            sp.dma_start(s_ea3[0:E, :].rearrange("(r q) c -> r (q c)", r=LONG_ROWS),
                         ea3.rearrange("(r q) c -> r (q c)", r=LONG_ROWS)).then_inc(copied, 16)
            sp.wait_ge(put, 5 * 16)
            sp.wait_ge(x_in, 2 * 16)
            sp.wait_ge(flag_ready, 1)
            sp.wait_ge(copied, 3 * 16)

        @block.gpsimd
        def _(pool):
            exact = dict(allow_small_or_imprecise_dtypes=True)
            nc.gpsimd.iota(col[:, :], [[1, P]], base=0, channel_multiplier=0, **exact).then_inc(iotas, 1)
            nc.gpsimd.iota(col2[:, :], [[0, 2], [1, P]], base=0, channel_multiplier=0, **exact).then_inc(iotas, 1)
            nc.gpsimd.iota(part[:, :], [[0, 1]], base=0, channel_multiplier=1, **exact).then_inc(iotas, 1)
            nc.gpsimd.iota(thr[:, :], [[P, NT]], base=P, channel_multiplier=0, **exact).then_inc(iotas, 1)
            pool.wait_ge(iotas, 4)

        @block.vector
        def _(dve):
            link = chained(dve, vec)
            nc.vector.memset(nxt_i[:, EP - 1:EP], PAD).then_inc(last_set, 1)
            for tile in clear:
                nc.vector.memset(tile, 0.0).then_inc(cleared, 1)
            nc.vector.memset(X[:, (NB - 1) * C:NB * C], 0.0).then_inc(pads, 1)
            nc.vector.memset(pad_i[:, :], PAD).then_inc(pads, 1)
            nc.vector.memset(zero_i[:, :], 0).then_inc(pads, 1)
            nc.vector.memset(zeros[:, :, 0:BW - 1], 0.0).then_inc(pads, 1)
            nc.vector.memset(zeros[:, :, BW - 1:BW], float(PAD)).then_inc(pads, 1)
            link(nc.vector.memset(ones[:, :], 1.0))
            link(nc.vector.memset(ones_b[:, :], 1.0))
            dve.wait_ge(iotas, 4)
            link(nc.vector.tensor_scalar(thr_h[:, :], thr[:, :], -0.5, None, ALU.add))
            link(nc.vector.tensor_scalar(ident[:, :], col[:, :], part[:, 0:1], None, ALU.is_equal))
            link(nc.vector.tensor_scalar(lower_b[:, :], col[:, :], part[:, 0:1], None, ALU.is_gt))
            link(nc.vector.tensor_scalar(upper_b[:, :], col[:, :], part[:, 0:1], None, ALU.is_le))
            link(nc.vector.tensor_scalar(valid[:, :], part[:, :], float(LAST), None, ALU.is_lt))
            dve.wait_ge(dst_in, 16)
            link(nc.vector.tensor_copy(dst_f, dst_i))
            dve.wait_ge(nxt_in, 2 * 16)
            link(nc.vector.tensor_tensor(junk, nxt_i, dst_i, ALU.is_lt))
            nc.vector.tensor_reduce(viol[:, :], junk, AX.X, ALU.add).then_inc(order_seen, 1)
            dve.wait_ge(found, 1)
            nc.vector.tensor_copy(flags[:, :], found_p[:, 0:1]).then_inc(flag_ready, 1)
            dve.wait_ge(src_in, 16)
            link(nc.vector.tensor_copy(src_f, src_i))
            dve.wait_ge(gaussians_in, 16 * len(gaussians))
            link(nc.vector.tensor_tensor(nis[:, :, :], nis[:, :, :], nis[:, :, :], ALU.mult))
            link(nc.vector.tensor_scalar(nis[:, :, :], nis[:, :, :], GMM_EPS, None, ALU.add))
            link(nc.vector.reciprocal(nis[:, :, :], nis[:, :, :]))
            link(nc.vector.tensor_scalar(nis[:, :, :], nis[:, :, :], -0.5, None, ALU.mult))

        @block.scalar
        def _(act):
            for to, of in gaussians:
                act.dma_start(to, of).then_inc(gaussians_in, 16)
            act.wait_ge(cleared, len(clear))
            for to, of in rest:
                act.dma_start(to, of).then_inc(weights_in, 16)
            act.wait_ge(gaussians_in, 16 * len(gaussians))

        @block.tensor
        def _(pe):
            pe.wait_ge(vec, 1)
            pe.wait_ge(order_seen, 1)
            nc.tensor.matmul(found_p[:, 0:1], ones[:, :], viol[:, :], start=True, stop=True).then_inc(found, 1)


def put_tables(sp, tab_i, tab_f, columns, column_f, rows, less_first, stored, reread):
    q = column_f.shape[1]
    for r, column in enumerate(columns):
        sp.dma_start(tab_i[r, :].rearrange("(p q) -> p q", q=q), column[:, :]).then_inc(stored, 16)
    sp.dma_start(tab_f[0, :].rearrange("(p q) -> p q", q=q), column_f[:, :]).then_inc(stored, 16)
    sp.wait_ge(stored, (len(columns) + 1) * 16)
    for r, row in enumerate(rows):
        sp.dma_start(row[:, :], tab_i[r:r + 1, :]).then_inc(reread, 16)
    sp.dma_start(less_first[:, :], tab_f[0:1, :].to_broadcast([P, less_first.shape[1]])).then_inc(reread, 16)
    sp.wait_ge(reread, (len(rows) + 1) * 16)


def put_turns(link, nc, loops, at, chunks, turn_i):
    link(nc.vector.tensor_scalar(turn_i[:, :], chunks, float(BUFS - 1), None, ALU.add))
    link(nc.vector.tensor_scalar(loops[:, at:at + 1], turn_i[:, :], BUFS.bit_length() - 1, None, ALU.arith_shift_right))
    link(nc.vector.tensor_scalar(loops[:, at + 1:at + 2], loops[:, at:at + 1], -1.0, None, ALU.add))
    link(nc.vector.tensor_scalar(loops[:, at + 2:at + 3], loops[:, at:at + 1], BUFS / 2, None, ALU.mult))
    link(nc.vector.tensor_scalar(loops[:, at + 3:at + 4], loops[:, at:at + 1], BUFS / 2, -1.0, ALU.mult, ALU.add))


def window_tables(nc, tag, s_dst, flags, ones, Z, tab_i, tab_f, rows, to_row, loops):
    CQ = table_chunks(CH) // P
    with ExitStack() as own:
        def sb1(name, shape, dt=FP32):
            return own.enter_context(nc.sbuf_tensor(f"{tag}_{name}", shape, dt))
        sem = Semaphores(nc, own, tag)
        ends = sb1("ends", [1, 2 * SEGS], I32)
        first_t, last_t = (ends[:, :].rearrange("o (s q) -> o s q", q=2)[:, :, n] for n in range(2))
        int_i, halves = (sb1(n, [1, SEGS], I32) for n in ("int_i", "halves"))
        by_block = sb1("by_block", [1, 1])
        begin, end, odd, zero = (Z[0:1, (CQ + n) * SEGS:(CQ + n + 1) * SEGS] for n in range(2, 6))
        upto_rise = sb1("upto_rise", [1, 2, SEGS])
        upto, rise = (Z[:, (CQ + n) * SEGS:(CQ + n + 1) * SEGS] for n in range(2))
        start = sb1("start", [1, SEGS])
        begin0 = sb1("begin0", [P, 1])
        turn_i = sb1("turn_i", [P, 1], I32)
        cid, seg, win, less_first, off = (sb1(n, [P, CQ]) for n in ("cid", "seg", "win", "less_first", "off"))
        off_i, win_i, lower_i, upper_i, shift_i = (sb1(n, [P, CQ], I32) for n in ("off_i", "win_i", "lower_i", "upper_i", "shift_i"))
        cmp = Z[:, 0:CQ * SEGS].rearrange("p (q s) -> p q s", s=SEGS)
        wide_p = [own.enter_context(nc.psum_tensor(f"{tag}_wide_p{n}", [P, 512], FP32)) for n in range(5)]
        iotas, read, vec, row_ready, spread, tables, stored, reread = (
            sem(n) for n in ("iotas", "read", "vec", "row_ready", "spread", "tables", "stored", "reread"))
        cuts = [(a, min(a + 512, SEGS)) for a in range(0, SEGS, 512)]
        block = own.enter_context(nc.Block())

        @block.sync
        def _(sp):
            pairs = s_dst[CH - 1:CH - 1 + (SEGS - 1) * CH].rearrange("(s q) -> s q", q=CH)[:, 0:2].unsqueeze(0)
            sp.dma_start(ends[:, 1:2 * SEGS - 1].rearrange("o (s q) -> o s q", q=2), pairs).then_inc(read, 16)
            sp.dma_start(ends[:, 0:1], s_dst[0:1].unsqueeze(0)).then_inc(read, 16)
            sp.dma_start(ends[:, 2 * SEGS - 1:2 * SEGS], s_dst[E - 1:E].unsqueeze(0)).then_inc(read, 16)
            sp.wait_ge(tables, 1)
            put_tables(sp, tab_i, tab_f, (off_i, lower_i, upper_i, shift_i), less_first, rows, to_row, stored, reread)

        @block.gpsimd
        def _(pool):
            nc.gpsimd.iota(cid[:, :], [[1, CQ]], base=0, channel_multiplier=CQ,
                           allow_small_or_imprecise_dtypes=True).then_inc(iotas, 1)

        @block.vector
        def _(dve):
            link = chained(dve, vec)
            SHIFT = HW.bit_length() - 1
            upto_r, rise_r = upto_rise[:, 0, :], upto_rise[:, 1, :]
            link(nc.vector.memset(zero[:, :], 0.0))
            link(nc.vector.tensor_scalar(by_block[:, :], flags[0:1, :], 1.0, None, ALU.min))
            dve.wait_ge(read, 3 * 16)
            link(nc.vector.tensor_scalar(halves[:, :], first_t, SHIFT, None, ALU.arith_shift_right))
            link(nc.vector.tensor_scalar(int_i[:, :], halves[:, :], 1, None, ALU.bitwise_and))
            link(nc.vector.tensor_scalar(odd[:, :], int_i[:, :], by_block[:, 0:1], None, ALU.mult))
            link(nc.vector.tensor_tensor(begin[:, :], halves[:, :], odd[:, :], ALU.subtract))
            link(nc.vector.tensor_scalar(halves[:, :], last_t, SHIFT, None, ALU.arith_shift_right))
            link(nc.vector.tensor_scalar(int_i[:, :], halves[:, :], 1, None, ALU.bitwise_and))
            link(nc.vector.tensor_scalar(odd[:, :], int_i[:, :], -1.0, 1.0, ALU.mult, ALU.add))
            link(nc.vector.tensor_scalar(odd[:, :], odd[:, :], by_block[:, 0:1], None, ALU.mult))
            link(nc.vector.tensor_tensor(end[:, :], halves[:, :], odd[:, :], ALU.add))
            link(nc.vector.tensor_tensor(halves[:, :], end[:, :], begin[:, :], ALU.subtract))
            link(nc.vector.tensor_scalar(int_i[:, :], halves[:, :], 1, None, ALU.arith_shift_right))
            link(nc.vector.tensor_scalar(odd[:, :], int_i[:, :], 1.0, None, ALU.add))
            link(nc.vector.tensor_tensor_scan(upto_r, odd[:, :], zero[:, :], 0.0, ALU.add, ALU.add))
            link(nc.vector.tensor_tensor(odd[:, :], upto_r, odd[:, :], ALU.subtract))
            link(nc.vector.scalar_tensor_tensor(start[:, :], odd[:, :], -2.0, begin[:, :], ALU.mult, ALU.add))
            link(nc.vector.memset(rise_r, 0.0))
            link(nc.vector.tensor_tensor(rise_r[:, 0:SEGS - 1], start[:, 1:SEGS], start[:, 0:SEGS - 1], ALU.subtract))
            nc.vector.tensor_copy(odd[:, 0:1], start[:, 0:1]).then_inc(row_ready, 1)
            dve.wait_ge(spread, 1)
            for n, (a, b) in enumerate(cuts):
                link(nc.vector.tensor_copy(upto[:, a:b], wide_p[n][:, 0:b - a]))
                link(nc.vector.tensor_copy(rise[:, a:b], wide_p[2 + n][:, 0:b - a]))
            link(nc.vector.tensor_copy(begin0[:, :], wide_p[4][:, 0:1]))
            put_turns(link, nc, loops, 0, upto[:, SEGS - 1:SEGS], turn_i)
            dve.wait_ge(iotas, 1)
            link(nc.vector.tensor_tensor(cmp, cid[:, :].unsqueeze(2).to_broadcast([P, CQ, SEGS]),
                                         upto[:, :].unsqueeze(1).to_broadcast([P, CQ, SEGS]), ALU.is_ge))
            link(nc.vector.tensor_reduce(seg[:, :], cmp, AX.X, ALU.add))
            link(nc.vector.tensor_tensor(cmp, cmp, rise[:, :].unsqueeze(1).to_broadcast([P, CQ, SEGS]), ALU.mult))
            link(nc.vector.tensor_reduce(win[:, :], cmp, AX.X, ALU.add))
            link(nc.vector.scalar_tensor_tensor(win[:, :], cid[:, :], 2.0, win[:, :], ALU.mult, ALU.add))
            link(nc.vector.tensor_scalar(win[:, :], win[:, :], begin0[:, 0:1], float(WINDOWS - 1), ALU.add, ALU.min))
            link(nc.vector.tensor_scalar(off[:, :], seg[:, :], float(CH), float(E), ALU.mult, ALU.min))
            link(nc.vector.tensor_copy(off_i[:, :], off[:, :]))
            link(nc.vector.tensor_scalar(less_first[:, :], win[:, :], -float(HW), None, ALU.mult))
            link(nc.vector.tensor_copy(win_i[:, :], win[:, :]))
            link(nc.vector.tensor_scalar(upper_i[:, :], win_i[:, :], 1, None, ALU.arith_shift_right))
            link(nc.vector.tensor_scalar(shift_i[:, :], win_i[:, :], 1, None, ALU.bitwise_and))
            link(nc.vector.tensor_tensor(lower_i[:, :], upper_i[:, :], shift_i[:, :], ALU.add))
            nc.vector.tensor_scalar(shift_i[:, :], shift_i[:, :], float(HW), None, ALU.mult).then_inc(tables, 1)

        @block.tensor
        def _(pe):
            pe.wait_ge(row_ready, 1)
            for r in range(2):
                for n, (a, b) in enumerate(cuts):
                    nc.tensor.matmul(wide_p[2 * r + n][:, 0:b - a], ones[0:1, :], upto_rise[:, r, a:b], start=True, stop=True)
            nc.tensor.matmul(wide_p[4][:, 0:1], ones[0:1, :], odd[:, 0:1], start=True, stop=True).then_inc(spread, 1)


def block_tables(nc, tag, below, first, col, ones, tab_i, tab_f, row_off, row_blk, to_row, loops):
    ch, CQ = CHS, table_chunks(CHS) // P
    with ExitStack() as own:
        def sb1(name, shape, dt=FP32):
            return own.enter_context(nc.sbuf_tensor(f"{tag}_{name}", shape, dt))
        sem = Semaphores(nc, own, tag)
        tot, num, nch, upto, cfirst, obase, zero = (sb1(n, [P, NB1]) for n in ("tot", "num", "nch", "upto", "cfirst", "obase", "zero"))
        num_i, num_j, turn_i = sb1("num_i", [P, NB1], I32), sb1("num_j", [P, NB1], I32), sb1("turn_i", [P, 1], I32)
        cid, blk, off, less_first = (sb1(n, [P, CQ]) for n in ("cid", "blk", "off", "less_first"))
        cmp = sb1("cmp", [P, CQ, NB1])
        blk_i, off_i = sb1("blk_i", [P, CQ], I32), sb1("off_i", [P, CQ], I32)
        total_p = own.enter_context(nc.psum_tensor(f"{tag}_total_p", [P, 512], FP32))
        iotas, halved, totals, vec, tables, stored, reread = (
            sem(n) for n in ("iotas", "halved", "totals", "vec", "tables", "stored", "reread"))
        block = own.enter_context(nc.Block())

        @block.sync
        def _(sp):
            sp.wait_ge(tables, 1)
            put_tables(sp, tab_i, tab_f, (off_i, blk_i), less_first, (row_off, row_blk), to_row, stored, reread)

        @block.gpsimd
        def _(pool):
            nc.gpsimd.iota(cid[:, :], [[1, CQ]], base=0, channel_multiplier=CQ,
                           allow_small_or_imprecise_dtypes=True).then_inc(iotas, 1)

        @block.vector
        def _(dve):
            link = chained(dve, vec)
            nc.vector.tensor_scalar(below[:, 0:NB1], below[:, 0:NB1], float(EP), 0.5, ALU.add, ALU.mult).then_inc(halved, 1)
            link(nc.vector.memset(zero[:, :], 0.0))
            link(nc.vector.memset(first[:, :], 0.0))
            link(nc.vector.memset(cfirst[:, :], 0.0))
            dve.wait_ge(iotas, 1)
            dve.wait_ge(totals, 1)
            link(nc.vector.tensor_copy(tot[:, :], total_p[:, 0:NB1]))
            link(nc.vector.tensor_copy(first[:, 1:NB1], tot[:, 0:NB]))
            link(nc.vector.tensor_tensor(num[:, :], tot[:, :], first[:, :], ALU.subtract))
            link(nc.vector.tensor_scalar(num_i[:, :], num[:, :], float(ch - 1), None, ALU.add))
            link(nc.vector.tensor_scalar(num_j[:, :], num_i[:, :], ch.bit_length() - 1, None, ALU.arith_shift_right))
            link(nc.vector.tensor_copy(nch[:, :], num_j[:, :]))
            link(nc.vector.tensor_tensor_scan(upto[:, :], nch[:, :], zero[:, :], 0.0, ALU.add, ALU.add))
            put_turns(link, nc, loops, 4, upto[:, NB1 - 1:NB1], turn_i)
            link(nc.vector.tensor_copy(cfirst[:, 1:NB1], upto[:, 0:NB]))
            link(nc.vector.scalar_tensor_tensor(obase[:, :], cfirst[:, :], -float(ch), first[:, :], ALU.mult, ALU.add))
            link(nc.vector.tensor_tensor(cmp[:, :, 0:NB], cid[:, :].unsqueeze(2).to_broadcast([P, CQ, NB]),
                                         upto[:, 0:NB].unsqueeze(1).to_broadcast([P, CQ, NB]), ALU.is_ge))
            link(nc.vector.tensor_reduce(blk[:, :], cmp[:, :, 0:NB], AX.X, ALU.add))
            link(nc.vector.tensor_scalar(less_first[:, :], blk[:, :], -float(P), None, ALU.mult))
            link(nc.vector.tensor_tensor(cmp[:, :, :], col[:, 0:NB1].unsqueeze(1).to_broadcast([P, CQ, NB1]),
                                         blk[:, :].unsqueeze(2).to_broadcast([P, CQ, NB1]), ALU.is_equal))
            link(nc.vector.tensor_tensor(cmp[:, :, :], cmp[:, :, :],
                                         obase[:, :].unsqueeze(1).to_broadcast([P, CQ, NB1]), ALU.mult))
            link(nc.vector.tensor_reduce(off[:, :], cmp[:, :, :], AX.X, ALU.add))
            link(nc.vector.scalar_tensor_tensor(off[:, :], cid[:, :], float(ch), off[:, :], ALU.mult, ALU.add))
            link(nc.vector.tensor_scalar(off_i[:, :], off[:, :], float(E), None, ALU.min))
            nc.vector.tensor_copy(blk_i[:, :], blk[:, :]).then_inc(tables, 1)

        @block.tensor
        def _(pe):
            pe.wait_ge(halved, 1)
            nc.tensor.matmul(total_p[:, 0:NB1], ones[:, :], below[:, 0:NB1], start=True, stop=True).then_inc(totals, 1)


def rank_edges(nc, rank_p, hot_s, tiles, lower_b, ones_b):
    more = dict(start=False, stop=True, skip_group_check=True)
    last = nc.tensor.matmul(rank_p[:, 0:tiles * NB], lower_b[:, :], hot_s, **more)
    for k in range(1, tiles):
        last = nc.tensor.matmul(rank_p[:, k * NB:tiles * NB], ones_b[:, :], hot_s[:, 0:(tiles - k) * NB], **more)
    return last


def complete_ranks(nc, rank_p, hot_s, tiles, upper_b, ones_b):
    more = dict(start=False, stop=True, skip_group_check=True)
    last = nc.tensor.matmul(rank_p[:, 0:tiles * NB], upper_b[:, :], hot_s, **more)
    for k in range(1, tiles):
        last = nc.tensor.matmul(rank_p[:, 0:(tiles - k) * NB], ones_b[:, :], hot_s[:, k * NB:tiles * NB], **more)
    return last


def order_edges(nc, go, src, dst, ea3, ea16, edges, flags, Z, below, thr, thr_h, first, col, ones, ones_b,
                lower_b, upper_b):
    dst_f, junk, junk_act = (Z[:, n * EP:(n + 1) * EP] for n in (3, 4, 5))
    HALF = NB1 // 2
    s_src, s_dst, s_ea3, s_ea16 = edges
    STEPS = E // (TR * P)
    with ExitStack() as own:
        def sb1(name, shape, dt=FP32):
            return own.enter_context(nc.sbuf_tensor(f"order_{name}", shape, dt))
        sem = Semaphores(nc, own, "order")
        srci, dsti, blki, idx = (sb1(n, [P, TR], I32) for n in ("srci", "dsti", "blki", "idx"))
        e3, e16 = sb1("e3", [P, TR, D3]), sb1("e16", [P, TR, EA])
        blkf = sb1("blkf", [P, TR])
        begin_row = sb1("begin_row", [1, TR, NB])
        hot_s = sb1("hot_s", [P, TR, NB], BF16)
        sel = sb1("sel", [P, TR, NB])
        rank_p = own.enter_context(nc.psum_tensor("order_rank_p", [P, 512], FP32))
        total_p = own.enter_context(nc.psum_tensor("order_total_p", [P, 512], FP32))
        counted, differed, halved, totals, firsts = (sem(n) for n in ("counted", "differed", "halved", "totals", "firsts"))
        begins, loaded, vec, hot_ready, ranked, selected, placed, completed = (sem(n) for n in (
            "begins", "loaded", "vec", "hot_ready", "ranked", "selected", "placed", "completed"))
        sent = sem.each("sent", 4)
        block = own.enter_context(nc.Block())

        def if_unordered(engine, body):
            flag = engine.value_load(flags[0:1, 0:1], min_val=0, max_val=E)
            with engine.If(flag > 0):
                body()
            with engine.Else():
                engine.sem_inc(go, 1)
            engine.sem_inc(go, 1)

        def steps(engine, step):
            step(0)
            with engine.Fori(1, STEPS) as i:
                step(i)

        @block.sync
        def _(sp):
            def load(i):
                if started(i):
                    for s in sent:
                        sp.wait_ge(s, i * (TR * 16))
                    plain(sp, go)
                at = bass.ds(i * (TR * P), TR * P)
                sp.dma_start(srci[:, :], src[at].rearrange("(p t) -> p t", t=TR)).then_inc(loaded, 16)
                sp.dma_start(dsti[:, :], dst[at].rearrange("(p t) -> p t", t=TR)).then_inc(loaded, 16)
                sp.dma_start(e3[:, :, :].rearrange("p t c -> p (t c)"), ea3[at, :].rearrange("(p t) c -> p (t c)", t=TR)).then_inc(loaded, 16)
                sp.dma_start(e16[:, :, :].rearrange("p t c -> p (t c)"), ea16[at, :].rearrange("(p t) c -> p (t c)", t=TR)).then_inc(loaded, 16)
            if_unordered(sp, lambda: steps(sp, load))

        @block.vector
        def _(dve):
            def place(i):
                dve.wait_ge(loaded, (i + 1) * 64)
                nc.vector.tensor_scalar(blki[:, :], dsti[:, :], P.bit_length() - 1, None, ALU.arith_shift_right).then_inc(vec, 1)
                dve.wait_ge(vec, 2 * i + 1)
                nc.vector.tensor_copy(blkf[:, :], blki[:, :]).then_inc(vec, 1)
                dve.wait_ge(vec, 2 * i + 2)
                if started(i):
                    dve.wait_ge(completed, i)
                nc.vector.tensor_tensor(hot_s[:, :, :], col[:, 0:NB].unsqueeze(1).to_broadcast([P, TR, NB]),
                                        blkf[:, :].unsqueeze(2).to_broadcast([P, TR, NB]), ALU.is_equal).then_inc(hot_ready, 1)
                dve.wait_ge(ranked, i + 1)
                nc.vector.tensor_tensor(sel[:, :, :], rank_p[:, 0:TR * NB].rearrange("p (t b) -> p t b", b=NB),
                                        hot_s[:, :, :], ALU.mult).then_inc(selected, 1)
                dve.wait_ge(selected, i + 1)
                nc.vector.tensor_reduce(blkf[:, :], sel[:, :, :], AX.X, ALU.add).then_inc(placed, 1)
                dve.wait_ge(placed, 2 * i + 1)
                nc.vector.tensor_copy(idx[:, :], blkf[:, :]).then_inc(placed, 1)

            def body():
                with dve.Fori(HALF, NB1) as b:
                    nc.vector.tensor_scalar(junk, dst_f, thr[:, bass.ds(b, 1)], None, ALU.is_lt, ALU.add,
                                            accum_out=below[:, bass.ds(b, 1)]).then_inc(counted, 1)
                    dve.wait_ge(counted, b - (HALF - 1))
                dve.wait_ge(differed, HALF)
                nc.vector.tensor_scalar(below[:, 0:HALF], below[:, 0:HALF], float(EP), 0.5, ALU.add, ALU.mult).then_inc(halved, 1)
                nc.vector.memset(first[:, :], 0.0).then_inc(firsts, 1)
                dve.wait_ge(totals, 1)
                dve.wait_ge(firsts, 1)
                nc.vector.tensor_copy(first[:, 1:NB1], total_p[:, 0:NB]).then_inc(firsts, 1)
                dve.wait_ge(firsts, 2)
                nc.vector.tensor_copy(begin_row[:, :, :], first[0:1, 0:NB].unsqueeze(1).to_broadcast([1, TR, NB])).then_inc(begins, 1)
                steps(dve, place)
            if_unordered(dve, body)

        @block.scalar
        def _(act):
            def body():
                with act.Fori(0, HALF) as b:
                    nc.scalar.activation(junk_act, dst_f, ACT.Sign, bias=thr_h[:, bass.ds(b, 1)], scale=-1.0,
                                         accum_out=below[:, bass.ds(b, 1)]).then_inc(differed, 1)
                    act.wait_ge(differed, b + 1)
            if_unordered(act, body)

        @block.tensor
        def _(pe):
            def rank(i):
                pe.wait_ge(hot_ready, i + 1)
                hs = hot_s[:, :, :].rearrange("p t b -> p (t b)")
                rank_edges(nc, rank_p, hs, TR, lower_b, ones_b).then_inc(ranked, 1)
                pe.wait_ge(selected, i + 1)
                complete_ranks(nc, rank_p, hs, TR, upper_b, ones_b).then_inc(completed, 1)

            def body():
                pe.wait_ge(halved, 1)
                nc.tensor.matmul(total_p[:, 0:NB1], ones[:, :], below[:, 0:NB1], start=True, stop=True).then_inc(totals, 1)
                pe.wait_ge(begins, 1)
                nc.tensor.matmul(rank_p[:, 0:TR * NB], ones[0:1, :], begin_row[:, :, :].rearrange("p t b -> p (t b)"),
                                 start=True, stop=True, skip_group_check=True)
                steps(pe, rank)
            if_unordered(pe, body)

        @block.gpsimd
        def _(pool):
            def send(i):
                pool.wait_ge(placed, 2 * i + 2)
                plain(pool, go)
                for j in range(TR):
                    for s, to, of in ((sent[0], s_src.unsqueeze(1), srci[:, j:j + 1]), (sent[1], s_dst.unsqueeze(1), dsti[:, j:j + 1]),
                                      (sent[2], s_ea3, e3[:, j, :]), (sent[3], s_ea16, e16[:, j, :])):
                        pool.indirect_dma_start(
                            out=to, out_offset=bass.IndirectOffsetOnAxis(ap=idx[:, j:j + 1].bitcast(U32), axis=0),
                            in_=of, in_offset=None).then_inc(s, 16)

            def body():
                steps(pool, send)
                for s in sent:
                    pool.wait_ge(s, STEPS * TR * 16)
            if_unordered(pool, body)


def weight_tiles(sb, w):
    K11 = 2 * KG + 1
    mu = sb("mu", [P, K11, D3])
    nis = sb("nis", [P, K11, D3])
    groups = [("L0_gnn_mu1", "L0_gnn_sigma1", 0, KG), ("L0_gnn_mus", "L0_gnn_sigmas", KG, 1),
              ("L0_gnn_mu2", "L0_gnn_sigma2", KG + 1, KG)]
    wt = {
        "w1a": sb("w1a", [P, MW]), "w1b": sb("w1b", [3 * C + 1, MW]),
        "w2a": sb("w2a", [P, MW]), "w2b": sb("w2b", [2 * C + 1, MW]),
        "gam1s": sb("gam1s", [P, 2 * C]), "bet1s": sb("bet1s", [P, 2 * C]),
        "gam2": sb("gam2", [P, C]), "bet2": sb("bet2", [P, C]),
        "wpq": sb("wpq", [C, 2 * H]), "wc": sb("wc", [P, T, 2 * H]),
        "wf2": sb("wf2", [H + 1, H]), "wn1": sb("wn1", [H, H]), "bn1": sb("bn1", [H, 1]),
        "wn2": sb("wn2", [H + 1, MW]),
    }
    loads = []

    def bcast(a):
        return a.unsqueeze(0).to_broadcast([P, a.shape[0]])
    for m, s, k, n in groups:
        loads.append((mu[:, k:k + n, :].rearrange("p k d -> p (k d)"), bcast(w[m].rearrange("k d -> (k d)"))))
        loads.append((nis[:, k:k + n, :].rearrange("p k d -> p (k d)"), bcast(w[s].rearrange("k d -> (k d)"))))
    for k in range(KG):
        for name, g in (("w1", "L0_gnn_g1"), ("w2", "L0_gnn_g2")):
            to = wt[name + "a"][k * C:(k + 1) * C, 0:C] if k < 4 else wt[name + "b"][0:C, 0:C]
            loads.append((to, w[g][:, k * C:(k + 1) * C]))
    loads += [
        (wt["w1b"][C:2 * C, C:2 * C], w["L0_gnn_gs"]),
        (wt["w1b"][2 * C:3 * C, 0:C], w["L0_gnn_root1"]), (wt["w1b"][2 * C:3 * C, C:2 * C], w["L0_gnn_roots"]),
        (wt["w1b"][3 * C:3 * C + 1, 0:C], w["L0_gnn_b1"].unsqueeze(0)),
        (wt["w1b"][3 * C:3 * C + 1, C:2 * C], w["L0_gnn_bs"].unsqueeze(0)),
        (wt["w2b"][C:2 * C, 0:C], w["L0_gnn_root2"]), (wt["w2b"][2 * C:2 * C + 1, 0:C], w["L0_gnn_b2"].unsqueeze(0)),
        (wt["gam1s"][:, 0:C], bcast(w["L0_gnn_gam1"])), (wt["gam1s"][:, C:2 * C], bcast(w["L0_gnn_gams"])),
        (wt["bet1s"][:, 0:C], bcast(w["L0_gnn_bet1"])), (wt["bet1s"][:, C:2 * C], bcast(w["L0_gnn_bets"])),
        (wt["gam2"][:, :], bcast(w["L0_gnn_gam2"])), (wt["bet2"][:, :], bcast(w["L0_gnn_bet2"])),
        (wt["wpq"][:, 0:H], w["L1_gnn_Wf1"][0:C, :]), (wt["wpq"][:, H:2 * H], w["L1_gnn_Wf1"][C:2 * C, :]),
        (wt["wf2"][0:H, :], w["L1_gnn_Wf2"]), (wt["wf2"][H:H + 1, :], w["L1_gnn_bf2"].unsqueeze(0)),
        (wt["wn1"][:, :], w["L1_gnn_Wn1"]), (wt["bn1"][:, :], w["L1_gnn_bn1"].unsqueeze(1)),
        (wt["wn2"][0:H, 0:C], w["L1_gnn_Wn2"]), (wt["wn2"][H:H + 1, 0:C], w["L1_gnn_bn2"].unsqueeze(0)),
    ]
    for j in range(T):
        for half in range(2):
            to = wt["wc"][j * C:j * C + EA, j, half * H:(half + 1) * H]
            loads.append((to, w["L1_gnn_Wf1"][2 * C:2 * C + EA, :]))
            loads.append((wt["wc"][j * C + EA:j * C + EA + 1, j, half * H:(half + 1) * H], w["L1_gnn_bf1"].unsqueeze(0)))
    clear = [wt[name][:, :] for name in ("w1a", "w1b", "w2a", "w2b", "wn2")] + [wt["wc"][:, :, :]]
    return mu, nis, wt, clear, loads


def turns_of(engine, loops, k, bufs=BUFS):
    least, most = (n * (BUFS // bufs) for n in (MIN_TURNS[k], MAX_TURNS[k]))
    at = 4 * k + (0 if bufs == BUFS else 2)
    n = engine.snap(engine.value_load(loops[0:1, at:at + 1], min_val=least, max_val=most))
    final = engine.snap(engine.value_load(loops[0:1, at + 1:at + 2], min_val=least - 1, max_val=most - 1))
    return n, final


def gmm_sums(nc, go, tag, edge_rows, table, K, with_count, mu, nis, k0, Z, col2, row_off, row_lower, row_upper, row_shift,
             less_first, loops, tally=None):
    s_src, s_dst, s_ea3 = edge_rows
    W = K * C + (1 if with_count else 0)
    with ExitStack() as own:
        def each(name, shape, dt=FP32):
            return [own.enter_context(nc.sbuf_tensor(f"{tag}_{name}{u}", shape, dt)) for u in range(BUFS)]

        sem = Semaphores(nc, own, tag)


        def sem2(name):
            return sem.each(name, BUFS)
        srci, dsti = each("srci", [P, T], I32), each("dsti", [P, T], I32)
        ea = each("ea", [P, T, D3])
        rows = each("rows", [P, T, C])
        lo = each("lo", [P, T])
        hot = each("hot", [P, T, P])
        dif, sq, sc = each("dif", [P, T, K, D3]), each("sq", [P, T, K, D3]), each("sc", [P, T, K, D3])
        logw, wgt = each("logw", [P, T, K]), each("wgt", [P, T, K])
        wx = each("wx", [P, T, W])
        agg = [own.enter_context(nc.psum_tensor(f"{tag}_agg{u}", [P, 512], FP32)) for u in range(BUFS)]
        loaded, gathered = sem2("loaded"), sem2("gathered")
        logw_ready, w_ready, wx_ready = sem2("logw_ready"), sem2("w_ready"), sem2("wx_ready")
        agg_done, added, cleared = sem2("agg_done"), sem2("added"), sem("cleared")
        dif_ready, lo_ready, sq_ready, sc_ready = (sem2(n) for n in ("dif_ready", "lo_ready", "sq_ready", "sc_ready"))
        tallied = sem("tallied")
        block = own.enter_context(nc.Block())

        @block.sync
        def _(sp):
            def load(i, u):
                off = sp.value_load(row_off[0:1, bass.ds(BUFS * i + u, 1)], min_val=0, max_val=E)
                if started(i):
                    sp.wait_ge(wx_ready[u], i)
                    sp.wait_ge(lo_ready[u], i)
                    plain(sp, go)
                sp.dma_start(srci[u][:, :], s_src[bass.ds(off, CH)].rearrange("(p t) -> p t", t=T)).then_inc(loaded[u], 16)
                sp.dma_start(dsti[u][:, :], s_dst[bass.ds(off, CH)].rearrange("(p t) -> p t", t=T)).then_inc(loaded[u], 16)
                sp.dma_start(ea[u][:, :, :].rearrange("p t d -> p (t d)"),
                             s_ea3[bass.ds(off, CH), :].rearrange("(p t) d -> p (t d)", t=T)).then_inc(loaded[u], 16)
            turns(sp, turns_of(sp, loops, 0), load, bufs=BUFS)

        @block.gpsimd
        def _(pool):
            def gather(i, u):
                pool.wait_ge(loaded[u], (i + 1) * 48)
                plain(pool, go)
                for j in range(T):
                    pool.indirect_dma_start(
                        out=rows[u][:, j, :], out_offset=None, in_=table[:, :],
                        in_offset=bass.IndirectOffsetOnAxis(ap=srci[u][:, j:j + 1].bitcast(U32), axis=0),
                    ).then_inc(gathered[u], 16)
            turns(pool, turns_of(pool, loops, 0), gather, bufs=BUFS)

        @block.vector
        def _(dve):
            link0 = chained(dve, cleared)
            link0(nc.vector.memset(Z[:, :], 0.0))
            if with_count:
                for u in range(BUFS):
                    link0(nc.vector.memset(wx[u][:, :, K * C:W], 1.0))

            def add(i, u):
                at = bass.ds(BUFS * i + u, 1)
                lower = dve.value_load(row_lower[0:1, at], min_val=0, max_val=NB)
                upper = dve.value_load(row_upper[0:1, at], min_val=0, max_val=NB)
                dve.wait_ge(agg_done[u], i + 1)
                if started(i) or u:
                    dve.wait_ge(added[u - 1], 2 * before(i, u, BUFS)[0] + 2)
                z = Z[0:HW, bass.ds(lower * ZW, W)]
                nc.vector.tensor_tensor(z, z, agg[u][0:HW, 0:W], ALU.add).then_inc(added[u], 1)
                z = Z[HW:P, bass.ds(upper * ZW, W)]
                nc.vector.tensor_tensor(z, z, agg[u][HW:P, 0:W], ALU.add).then_inc(added[u], 1)

            def multiply(i, u):
                dve.wait_ge(gathered[u], (i + 1) * 16 * T)
                dve.wait_ge(w_ready[u], i + 1)
                nc.vector.tensor_tensor(wx[u][:, :, 0:K * C].rearrange("p t (k c) -> p t k c", c=C),
                                        rows[u][:, :, :].unsqueeze(2).to_broadcast([P, T, K, C]),
                                        wgt[u][:, :, :].unsqueeze(3).to_broadcast([P, T, K, C]), ALU.mult).then_inc(wx_ready[u], 1)

            def weigh(i, u):
                dve.wait_ge(loaded[u], (i + 1) * 48)
                nc.vector.tensor_tensor(dif[u][:, :, :, :], ea[u][:, :, :].unsqueeze(2).to_broadcast([P, T, K, D3]),
                                        mu[:, k0:k0 + K, :].unsqueeze(1).to_broadcast([P, T, K, D3]), ALU.subtract).then_inc(dif_ready[u], 1)
                if started(i) or u >= 2:
                    add(*earlier(i, u, 2, BUFS))
                dve.wait_ge(dif_ready[u], i + 1)
                nc.vector.tensor_tensor(sq[u][:, :, :, :], dif[u][:, :, :, :], dif[u][:, :, :, :], ALU.mult).then_inc(sq_ready[u], 1)
                if started(i) or u:
                    multiply(*before(i, u, BUFS))
                dve.wait_ge(sq_ready[u], i + 1)
                nc.vector.tensor_tensor(sc[u][:, :, :, :], sq[u][:, :, :, :],
                                        nis[:, k0:k0 + K, :].unsqueeze(1).to_broadcast([P, T, K, D3]), ALU.mult).then_inc(sc_ready[u], 1)
                shift = dve.value_load(row_shift[0:1, bass.ds(BUFS * i + u, 1)], min_val=0, max_val=HW)
                dve.wait_ge(lo_ready[u], i + 1)
                if started(i):
                    dve.wait_ge(agg_done[u], i)
                nc.vector.tensor_tensor(hot[u][:, :, :], col2[:, bass.ds(shift, P)].unsqueeze(1).to_broadcast([P, T, P]),
                                        lo[u][:, :].unsqueeze(2).to_broadcast([P, T, P]), ALU.is_equal)
                dve.wait_ge(sc_ready[u], i + 1)
                nc.vector.tensor_reduce(logw[u][:, :, :], sc[u][:, :, :, :], AX.X, ALU.add).then_inc(logw_ready[u], 1)

            def finish(i, u):
                multiply(i, u)
                add(i, u - 1)
                add(i, u)
            turns(dve, turns_of(dve, loops, 0), weigh, finish, bufs=BUFS)

        @block.scalar
        def _(act):
            def exponent(i, u):
                act.wait_ge(loaded[u], (i + 1) * 48)
                if started(i):
                    act.wait_ge(logw_ready[u], i)
                nc.scalar.activation(lo[u][:, :], dsti[u][:, :], ACT.Identity, bias=less_first[:, bass.ds(BUFS * i + u, 1)]).then_inc(lo_ready[u], 1)
                if tally is not None and u == 0:
                    src_f, junk, thr, diff = tally
                    if started(i):
                        act.wait_ge(tallied, i)
                    nc.scalar.activation(junk, src_f, ACT.Sign, bias=thr[:, bass.ds(i, 1)], scale=-1.0,
                                         accum_out=diff[:, bass.ds(i, 1)]).then_inc(tallied, 1)
                act.wait_ge(logw_ready[u], i + 1)
                nc.scalar.activation(wgt[u][:, :, :], logw[u][:, :, :], ACT.Exp).then_inc(w_ready[u], 1)
            turns(act, turns_of(act, loops, 0), exponent, bufs=BUFS)

        @block.tensor
        def _(pe):
            def scatter(i, u):
                pe.wait_ge(wx_ready[u], i + 1)
                if started(i):
                    pe.wait_ge(added[u], 2 * i)
                for j in range(T):
                    last = nc.tensor.matmul(agg[u][:, 0:W], hot[u][:, j, :], wx[u][:, j, :], start=(j == 0), stop=(j == T - 1))
                last.then_inc(agg_done[u], 1)
            turns(pe, turns_of(pe, loops, 0), scatter, bufs=BUFS)


def counts(nc, tag, Z, RC, weights_in, weight_loads, ea16, s_ea16, flags, ea16_copied):
    with ExitStack() as own:
        sem = Semaphores(nc, own, tag)
        vec = sem("vec")
        block = own.enter_context(nc.Block())

        @block.sync
        def _(sp):
            out_of_order = sp.value_load(flags[0:1, 0:1], min_val=0, max_val=E)
            with sp.If(out_of_order == 0):
                sp.dma_start(s_ea16[0:E, :].rearrange("(r q) c -> r (q c)", r=LONG_ROWS),
                             ea16.rearrange("(r q) c -> r (q c)", r=LONG_ROWS)).then_inc(ea16_copied, 16)
            with sp.Else():
                sp.sem_inc(ea16_copied, 16)

        @block.vector
        def _(dve):
            link = chained(dve, vec)
            cnt = Z[:, 0:NB * ZW].rearrange("p (b w) -> p b w", w=ZW)[:, :, ZW - 1]
            link(nc.vector.tensor_scalar(RC[:, :], cnt, 1.0, None, ALU.max))
            dve.wait_ge(weights_in, 16 * weight_loads)
            link(nc.vector.reciprocal(RC[:, :], RC[:, :]))


def node_products(nc, tag, parts, with_one, weights, OW, dest, dpitch, ident):
    width = sum(p[2] for p in parts) + int(with_one)
    cuts = [(a, min(a + P, width)) for a in range(0, width, P)]
    OUT = 2 * P
    with ExitStack() as own:
        def each(name, shape, dt=FP32, make=None):
            return [own.enter_context((make or nc.sbuf_tensor)(f"{tag}_{name}{u}", shape, dt)) for u in range(NBUFS)]
        sem = Semaphores(nc, own, tag)
        stage = each("stage", [P, width])
        turned = each("turned", [P, len(cuts), P])
        bank = each("bank", [P, 512], make=nc.psum_tensor)
        staged, transposed, copied, done, saved = (sem.each(s, NBUFS) for s in ("staged", "transposed", "copied", "done", "saved"))
        one_set = sem("one_set")
        block = own.enter_context(nc.Block())
        starts = [sum(p[2] for p in parts[:n]) for n in range(len(parts))]

        @block.gpsimd
        def _(pool):
            def put_second(i, u):
                if started(i):
                    pool.wait_ge(transposed[u], i)
                t, pitch, n, _ = parts[1]
                nc.gpsimd.tensor_copy(stage[u][:, starts[1]:starts[1] + n],
                                      t[:, bass.ds((NBUFS * i + u) * pitch, n)]).then_inc(staged[u], 1)
            if len(parts) > 1:
                turns(pool, NB // NBUFS, put_second, bufs=NBUFS)

        @block.vector
        def _(dve):
            if with_one:
                for u in range(NBUFS):
                    nc.vector.memset(stage[u][:, width - 1:width], 1.0).then_inc(one_set, 1)

            def save(i, u):
                dve.wait_ge(done[u], i + 1)
                nc.vector.tensor_copy(dest[:, bass.ds((NBUFS * i + u) * dpitch, OW)], bank[u][:, OUT:OUT + OW]).then_inc(saved[u], 1)

            def put_first(i, u):
                if started(i):
                    dve.wait_ge(transposed[u], i)
                t, pitch, n, scale = parts[0]
                from_ = t[:, bass.ds((NBUFS * i + u) * pitch, n)]
                if scale is None:
                    nc.vector.tensor_copy(stage[u][:, 0:n], from_).then_inc(staged[u], 1)
                else:
                    nc.vector.tensor_scalar(stage[u][:, 0:n], from_, scale[:, bass.ds(NBUFS * i + u, 1)], None, ALU.mult).then_inc(staged[u], 1)
                if started(i) or u >= 2:
                    save(*earlier(i, u, 2))

            def rest(i, u):
                save(i, u - 1)
                save(i, u)
            turns(dve, NB // NBUFS, put_first, rest, NBUFS)

        @block.scalar
        def _(act):
            def copy(i, u):
                act.wait_ge(transposed[u], i + 1)
                if started(i):
                    act.wait_ge(done[u], i)
                for n, (a, b) in enumerate(cuts):
                    nc.scalar.activation(turned[u][0:b - a, n, :], bank[u][0:b - a, n * P:(n + 1) * P], ACT.Copy).then_inc(copied[u], 1)
            turns(act, NB // NBUFS, copy, bufs=NBUFS)

        @block.tensor
        def _(pe):
            def multiply(i, u):
                pe.wait_ge(copied[u], (i + 1) * len(cuts))
                if started(i):
                    pe.wait_ge(saved[u], i)
                for n, (a, b) in enumerate(cuts):
                    wn = weights[n][0:b - a, :]
                    last = nc.tensor.matmul(bank[u][:, OUT:OUT + wn.shape[1]], turned[u][0:b - a, n, :], wn,
                                            start=(n == 0), stop=(n == len(cuts) - 1))
                last.then_inc(done[u], 1)

            def transpose(i, u):
                pe.wait_ge(staged[u], (i + 1) * len(parts))
                if with_one and not started(i):
                    pe.wait_ge(one_set, NBUFS)
                if started(i):
                    pe.wait_ge(copied[u], i * len(cuts))
                for n, (a, b) in enumerate(cuts):
                    last = nc.tensor.transpose(bank[u][0:b - a, n * P:(n + 1) * P], stage[u][:, a:b], ident[:, :])
                last.then_inc(transposed[u], 1)
                if started(i) or u:
                    multiply(*earlier(i, u, 1))
            turns(pe, NB // NBUFS, transpose, multiply, NBUFS)


def batch_norm(nc, tag, Y, pitch, c0, W, tmp, ones, valid, gamma, beta):
    Yv = Y[:, 0:NB * pitch].rearrange("p (b c) -> p b c", c=pitch)[:, :, c0:c0 + W]
    sqv = tmp[:, 0:NB * W].rearrange("p (b c) -> p b c", c=W)
    with ExitStack() as own:
        def one(name, shape=None):
            return own.enter_context(nc.sbuf_tensor(f"{tag}_{name}", shape or [P, W], FP32))

        sem = Semaphores(nc, own, tag)
        part_sum, part_sq, mean, var, sd, amp = (one(n) for n in ("part_sum", "part_sq", "mean", "var", "sd", "amp"))
        total = own.enter_context(nc.psum_tensor(f"{tag}_total", [P, 512], FP32))
        total2 = own.enter_context(nc.psum_tensor(f"{tag}_total2", [P, 512], FP32))
        vec, summed, mean_ready, squares, var_sum, var_ready, rooted = (
            sem(n) for n in ("vec", "summed", "mean_ready", "squares", "var_sum", "var_ready", "rooted"))
        block = own.enter_context(nc.Block())

        def over(a):
            return a[:, 0:W].unsqueeze(1).to_broadcast([P, NB, W])

        @block.vector
        def _(dve):
            link = chained(dve, vec)
            link(nc.vector.tensor_scalar(Yv[:, NB - 1, :], Yv[:, NB - 1, :], valid[:, 0:1], None, ALU.mult))
            nc.vector.tensor_reduce(part_sum[:, :], Yv.rearrange("p b c -> p c b"), AX.X, ALU.add).then_inc(summed, 1)
            dve.wait_ge(mean_ready, 1)
            link(nc.vector.tensor_scalar(mean[:, :], total[:, 0:W], 1.0 / N, None, ALU.mult))
            link(nc.vector.tensor_tensor(Yv, Yv, over(mean), ALU.subtract))
            link(nc.vector.tensor_scalar(Yv[:, NB - 1, :], Yv[:, NB - 1, :], valid[:, 0:1], None, ALU.mult))
            link(nc.vector.tensor_tensor(sqv, Yv, Yv, ALU.mult))
            nc.vector.tensor_reduce(part_sq[:, :], sqv.rearrange("p b c -> p c b"), AX.X, ALU.add).then_inc(squares, 1)
            dve.wait_ge(var_sum, 1)
            nc.vector.tensor_scalar(var[:, :], total2[:, 0:W], 1.0 / N, BN_EPS, ALU.mult, ALU.add).then_inc(var_ready, 1)
            dve.wait_ge(rooted, 1)
            link(nc.vector.reciprocal(amp[:, :], sd[:, :]))
            link(nc.vector.tensor_tensor(amp[:, :], amp[:, :], gamma[:, 0:W], ALU.mult))
            link(nc.vector.tensor_tensor(Yv, Yv, over(amp), ALU.mult))
            link(nc.vector.tensor_tensor(Yv, Yv, over(beta), ALU.add))

        @block.tensor
        def _(pe):
            pe.wait_ge(summed, 1)
            nc.tensor.matmul(total[:, 0:W], ones[:, :], part_sum[:, :], start=True, stop=True).then_inc(mean_ready, 1)
            pe.wait_ge(squares, 1)
            nc.tensor.matmul(total2[:, 0:W], ones[:, :], part_sq[:, :], start=True, stop=True).then_inc(var_sum, 1)

        @block.scalar
        def _(act):
            act.wait_ge(var_ready, 1)
            nc.scalar.activation(sd[:, :], var[:, :], ACT.Sqrt).then_inc(rooted, 1)


def by_block(a, w, pitch=None, n=NB):
    return a[:, 0:n * (pitch or w)].rearrange("p (b c) -> p b c", c=pitch or w)[:, :, 0:w]


def elu_rows(nc, tag, Y, pitch, HT, valid, tmp, h_dram):
    Yv, Hv = by_block(Y, C, pitch), by_block(HT, C)
    low = by_block(tmp, C)
    ex = tmp[:, NB * C:2 * NB * C].rearrange("p (b c) -> p b c", c=C)
    with ExitStack() as own:
        sem = Semaphores(nc, own, tag)
        vec, low_ready, ex_ready, h_ready, stored = (sem(n) for n in ("vec", "low_ready", "ex_ready", "h_ready", "stored"))
        block = own.enter_context(nc.Block())

        @block.vector
        def _(dve):
            link = chained(dve, vec)
            nc.vector.tensor_scalar(low, Yv, 0.0, None, ALU.min).then_inc(low_ready, 1)
            link(nc.vector.tensor_scalar(Hv, Yv, 0.0, -1.0, ALU.max, ALU.add))
            dve.wait_ge(ex_ready, 1)
            link(nc.vector.tensor_tensor(Hv, Hv, ex, ALU.add))
            nc.vector.tensor_scalar(Hv[:, NB - 1, :], Hv[:, NB - 1, :], valid[:, 0:1], None, ALU.mult).then_inc(h_ready, 1)

        @block.scalar
        def _(act):
            act.wait_ge(low_ready, 1)
            nc.scalar.activation(ex, low, ACT.Exp).then_inc(ex_ready, 1)

        @block.sync
        def _(sp):
            sp.wait_ge(h_ready, 1)
            sp.dma_start(h_dram.rearrange("(b p) c -> p b c", p=P), Hv).then_inc(stored, 16)
            sp.wait_ge(stored, 16)


def norm_steps(nc, dve, link, Xv, sqv, stat, var_ready, rooted, sd):
    def over(a):
        return a[:, :].unsqueeze(2).to_broadcast([P, NB, C])
    link(nc.vector.tensor_reduce(stat[:, :], Xv, AX.X, ALU.add))
    link(nc.vector.tensor_scalar(stat[:, :], stat[:, :], 1.0 / C, None, ALU.mult))
    link(nc.vector.tensor_tensor(Xv, Xv, over(stat), ALU.subtract))
    link(nc.vector.tensor_tensor(sqv, Xv, Xv, ALU.mult))
    link(nc.vector.tensor_reduce(stat[:, :], sqv, AX.X, ALU.add))
    nc.vector.tensor_scalar(stat[:, :], stat[:, :], 1.0 / C, LN_EPS, ALU.mult, ALU.add).then_inc(var_ready, 1)
    dve.wait_ge(rooted, 1)
    link(nc.vector.reciprocal(stat[:, :], sd[:, :]))
    return nc.vector.tensor_tensor(Xv, Xv, over(stat), ALU.mult)


def add_and_norm(nc, tag, Y, X, tmp):
    hv = by_block(Y, C, 2 * C)
    sv = Y[:, 0:NB * 2 * C].rearrange("p (b c) -> p b c", c=2 * C)[:, :, C:2 * C]
    Xv, low = by_block(X, C), by_block(tmp, C)
    ex = tmp[:, NB * C:2 * NB * C].rearrange("p (b c) -> p b c", c=C)
    with ExitStack() as own:
        sem = Semaphores(nc, own, tag)
        stat = own.enter_context(nc.sbuf_tensor(f"{tag}_stat", [P, NB], FP32))
        sd = own.enter_context(nc.sbuf_tensor(f"{tag}_sd", [P, NB], FP32))
        vec, low_ready, ex_ready, var_ready, rooted = (sem(n) for n in ("vec", "low_ready", "ex_ready", "var_ready", "rooted"))
        block = own.enter_context(nc.Block())

        @block.vector
        def _(dve):
            link = chained(dve, vec)
            link(nc.vector.tensor_tensor(hv, hv, sv, ALU.add))
            nc.vector.tensor_scalar(low, hv, 0.0, None, ALU.min).then_inc(low_ready, 1)
            link(nc.vector.tensor_scalar(hv, hv, 0.0, -1.0, ALU.max, ALU.add))
            link(nc.vector.tensor_tensor(Xv, Xv, hv, ALU.add))
            dve.wait_ge(ex_ready, 1)
            link(nc.vector.tensor_tensor(Xv, Xv, ex, ALU.add))
            link(norm_steps(nc, dve, link, Xv, low, stat, var_ready, rooted, sd))

        @block.scalar
        def _(act):
            act.wait_ge(low_ready, 1)
            nc.scalar.activation(ex, low, ACT.Exp).then_inc(ex_ready, 1)
            act.wait_ge(var_ready, 1)
            nc.scalar.activation(sd[:, :], stat[:, :], ACT.Sqrt).then_inc(rooted, 1)


def final_norm(nc, tag, X, tmp, out):
    Xv, sqv = by_block(X, C), by_block(tmp, C)
    with ExitStack() as own:
        sem = Semaphores(nc, own, tag)
        stat = own.enter_context(nc.sbuf_tensor(f"{tag}_stat", [P, NB], FP32))
        sd = own.enter_context(nc.sbuf_tensor(f"{tag}_sd", [P, NB], FP32))
        vec, var_ready, rooted, ready, written = (sem(n) for n in ("vec", "var_ready", "rooted", "ready", "written"))
        block = own.enter_context(nc.Block())

        @block.vector
        def _(dve):
            norm_steps(nc, dve, chained(dve, vec), Xv, sqv, stat, var_ready, rooted, sd).then_inc(ready, 1)

        @block.scalar
        def _(act):
            act.wait_ge(var_ready, 1)
            nc.scalar.activation(sd[:, :], stat[:, :], ACT.Sqrt).then_inc(rooted, 1)

        @block.sync
        def _(sp):
            sp.wait_ge(ready, 1)
            sp.dma_start(out[0:(NB - 1) * P, :].rearrange("(b p) c -> p b c", p=P), Xv[:, 0:NB - 1, :]).then_inc(written, 16)
            sp.dma_start(out[(NB - 1) * P:N, :], Xv[0:LAST, NB - 1, :]).then_inc(written, 16)
            sp.wait_ge(written, 2 * 16)


def pq_rows(nc, tag, PQ, qp_dram, F):
    PQv = by_block(PQ, 2 * H)
    with ExitStack() as own:
        sem = Semaphores(nc, own, tag)
        stored = sem("stored")
        cleared = sem("cleared")
        block = own.enter_context(nc.Block())

        @block.sync
        def _(sp):
            to = qp_dram.rearrange("(b p) c -> p b c", p=P)
            sp.dma_start(to[:, :, 0:H], PQv[:, :, H:2 * H]).then_inc(stored, 16)
            sp.dma_start(to[:, :, H:2 * H], PQv[:, :, 0:H]).then_inc(stored, 16)
            sp.wait_ge(stored, 32)

        @block.vector
        def _(dve):
            nc.vector.memset(F[:, :], 0.0).then_inc(cleared, 1)
            nc.vector.memset(PQ[:, NB * 2 * H:NB1 * 2 * H], 0.0).then_inc(cleared, 1)
            dve.wait_ge(cleared, 2)


def flow(nc, go, tag, s_src, s_dst, s_ea16, qp_dram, bwd_dram, PQ, F, wt, ident, col, col2, ones, ones_b,
         lower_b, upper_b, first, ea16_copied, row_off, row_lower, row_upper, row_shift, less_first, loops):
    with ExitStack() as own:
        def two(name, shape, dt=FP32, make=None):
            return [own.enter_context((make or nc.sbuf_tensor)(f"{tag}_{name}{u}", shape, dt)) for u in range(2)]

        sem = Semaphores(nc, own, tag)

        sem2 = sem.each
        srci, dsti, blki = two("srci", [P, T], I32), two("dsti", [P, T], I32), two("blki", [P, T], I32)
        ea = two("ea", [P, T, C])
        qp = two("qp", [P, T, 2 * H])
        lo, m1, m, hm, srcf = (two(n, [P, T]) for n in ("lo", "m1", "m", "hm", "srcf"))
        hot = two("hot", [P, T, P])
        hot_s = two("hot_s", [P, T, NB], BF16)
        sel = two("sel", [P, T, NB])
        pos, miss = two("pos", [P, T]), two("miss", [P, T])
        idx = two("idx", [P, T], I32)
        hot_t = two("hot_t", [P, T, P])
        ea_t = two("ea_t", [P, P])
        pq_win = two("pq_win", [P, 2 * H])
        fwd = two("fwd", [P, T, FW])
        bwd = two("bwd", [P, T, BW])
        rank_p = own.enter_context(nc.psum_tensor(f"{tag}_rank_p", [P, 512], FP32))
        hot_p = own.enter_context(nc.psum_tensor(f"{tag}_hot_p", [P, 512], FP32))
        ea_p = own.enter_context(nc.psum_tensor(f"{tag}_ea_p", [P, 512], FP32))
        hid_p = two("hid_p", [P, 512], make=nc.psum_tensor)
        sum_p = two("sum_p", [P, 512], make=nc.psum_tensor)
        (loaded, gathered, keys_read, ea_turned, hot_s_ready, hot_ready, hot_turned, turned_out, hid_done,
         relu_done, fwd_done, added, idx_ready, sent, ranked, rank_read) = (sem2(n) for n in (
             "loaded", "gathered", "keys_read", "ea_turned", "hot_s_ready", "hot_ready", "hot_turned", "turned_out",
             "hid_done", "relu_done", "fwd_done", "added", "idx_ready", "sent", "ranked", "rank_read"))
        vec, init = sem("vec"), sem("init")
        begin_row = own.enter_context(nc.sbuf_tensor(f"{tag}_begin_row", [1, T, NB], FP32))
        INIT = 9
        block = own.enter_context(nc.Block())

        @block.sync
        def _(sp):
            sp.wait_ge(init, INIT)

            def load(i, u):
                off = sp.value_load(row_off[0:1, bass.ds(2 * i + u, 1)], min_val=0, max_val=E)
                if started(i):
                    sp.wait_ge(keys_read[u], i)
                    sp.wait_ge(gathered[u], i * 16 * T)
                    sp.wait_ge(ea_turned[u], i)
                    plain(sp, go)
                sp.dma_start(srci[u][:, :], s_src[bass.ds(off, CH)].rearrange("(p t) -> p t", t=T)).then_inc(loaded[u], 16)
                sp.dma_start(dsti[u][:, :], s_dst[bass.ds(off, CH)].rearrange("(p t) -> p t", t=T)).then_inc(loaded[u], 16)
                sp.dma_start(ea[u][:, :, 0:EA], s_ea16[bass.ds(off, CH), :].rearrange("(p t) d -> p t d", t=T)).then_inc(loaded[u], 16)
            sp.wait_ge(ea16_copied, 16)
            turns(sp, turns_of(sp, loops, 0, 2), load)

        @block.gpsimd
        def _(pool):
            def send(i, u):
                pool.wait_ge(relu_done[u], (i + 1) * 3)
                pool.wait_ge(idx_ready[u], i + 1)
                plain(pool, go)
                for j in range(T):
                    pool.indirect_dma_start(
                        out=bwd_dram[:, :], out_offset=bass.IndirectOffsetOnAxis(ap=idx[u][:, j:j + 1].bitcast(U32), axis=0),
                        in_=bwd[u][:, j, :], in_offset=None, bounds_check=E - 1, oob_is_err=False,
                    ).then_inc(sent[u], 16)

            def gather(i, u):
                pool.wait_ge(loaded[u], (i + 1) * 48)
                if started(i):
                    pool.wait_ge(hid_done[u], i)
                plain(pool, go)
                for j in range(T):
                    pool.indirect_dma_start(
                        out=qp[u][:, j, :], out_offset=None, in_=qp_dram[:, :],
                        in_offset=bass.IndirectOffsetOnAxis(ap=srci[u][:, j:j + 1].bitcast(U32), axis=0),
                    ).then_inc(gathered[u], 16)
                if started(i) or u:
                    send(*before(i, u))
            n = turns_of(pool, loops, 0, 2)
            turns(pool, n, gather, send)
            for u in range(2):
                pool.wait_ge(sent[u], n[0] * (16 * T))

        @block.vector
        def _(dve):
            begin, link = looped(dve, vec, 7)
            nc.vector.tensor_copy(begin_row[:, :, :], first[0:1, 0:NB].unsqueeze(1).to_broadcast([1, T, NB])).then_inc(init, 1)
            for u in range(2):
                nc.vector.memset(ea[u][:, :, :], 0.0).then_inc(init, 1)
                dve.wait_ge(init, 4 * u + 2)
                nc.vector.memset(ea[u][:, :, EA:EA + 1], 1.0).then_inc(init, 1)
                nc.vector.memset(bwd[u][:, :, H:H + 1], 1.0).then_inc(init, 1)
                nc.vector.memset(fwd[u][:, :, H:FW], 1.0).then_inc(init, 1)

            def add(i, u):
                at = bass.ds(2 * i + u, 1)
                lower = dve.value_load(row_lower[0:1, at], min_val=0, max_val=NB)
                upper = dve.value_load(row_upper[0:1, at], min_val=0, max_val=NB)
                dve.wait_ge(fwd_done[u], i + 1)
                if started(i) or u:
                    dve.wait_ge(added[1 - u], 2 * before(i, u)[0] + 2)
                f = F[:, bass.ds(lower * P, HW)]
                nc.vector.tensor_tensor(f, f, sum_p[u][0:FW, 0:HW], ALU.add).then_inc(added[u], 1)
                f = F[:, bass.ds(upper * P + HW, HW)]
                nc.vector.tensor_tensor(f, f, sum_p[u][0:FW, HW:P], ALU.add).then_inc(added[u], 1)

            def keys(i, u):
                begin(i, u)
                dve.wait_ge(loaded[u], (i + 1) * 48)
                link(nc.vector.tensor_scalar(lo[u][:, :], dsti[u][:, :], less_first[:, bass.ds(2 * i + u, 1)], None, ALU.add))
                link(nc.vector.tensor_scalar(m1[u][:, :], lo[u][:, :], 0.0, None, ALU.is_ge))
                link(nc.vector.scalar_tensor_tensor(m[u][:, :], lo[u][:, :], float(P), m1[u][:, :], ALU.is_lt, ALU.mult))
                link(nc.vector.tensor_scalar(blki[u][:, :], srci[u][:, :], P.bit_length() - 1, None, ALU.arith_shift_right))
                link(nc.vector.scalar_tensor_tensor(hm[u][:, :], blki[u][:, :], 1.0, m[u][:, :], ALU.add, ALU.mult))
                if started(i):
                    dve.wait_ge(relu_done[u], i * 3)
                nc.vector.tensor_copy(srcf[u][:, :], srci[u][:, :]).then_inc(keys_read[u], 1)
                if started(i):
                    dve.wait_ge(ranked[u], 2 * i)
                nc.vector.tensor_tensor(hot_s[u][:, :, :], col[:, 1:NB + 1].unsqueeze(1).to_broadcast([P, T, NB]),
                                        hm[u][:, :].unsqueeze(2).to_broadcast([P, T, NB]), ALU.is_equal).then_inc(hot_s_ready[u], 1)
                if started(i):
                    dve.wait_ge(fwd_done[u], i)
                shift = dve.value_load(row_shift[0:1, bass.ds(2 * i + u, 1)], min_val=0, max_val=HW)
                nc.vector.tensor_tensor(hot[u][:, :, :], col2[:, bass.ds(shift, P)].unsqueeze(1).to_broadcast([P, T, P]),
                                        lo[u][:, :].unsqueeze(2).to_broadcast([P, T, P]), ALU.is_equal).then_inc(hot_ready[u], 1)
                dve.wait_ge(ranked[u], 2 * i + 1)
                nc.vector.tensor_tensor(sel[u][:, :, :], rank_p[:, 0:T * NB].rearrange("p (t b) -> p t b", b=NB),
                                        hot_s[u][:, :, :], ALU.mult).then_inc(rank_read[u], 1)
                dve.wait_ge(rank_read[u], i + 1)
                link(nc.vector.tensor_reduce(pos[u][:, :], sel[u][:, :, :], AX.X, ALU.add))
                link(nc.vector.tensor_scalar(miss[u][:, :], m[u][:, :], -float(PAD), float(PAD), ALU.mult, ALU.add))
                if started(i):
                    dve.wait_ge(sent[u], i * 16 * T)
                nc.vector.tensor_tensor(idx[u][:, :], pos[u][:, :], miss[u][:, :], ALU.add).then_inc(idx_ready[u], 1)
                if started(i) or u:
                    add(*before(i, u))
            turns(dve, turns_of(dve, loops, 0, 2), keys, add)

        @block.scalar
        def _(act):
            act.wait_ge(init, INIT)

            def relus(i, u):
                act.wait_ge(hid_done[u], i + 1)
                if started(i):
                    act.wait_ge(fwd_done[u], i)
                    act.wait_ge(sent[u], i * 16 * T)
                hid = hid_p[u][:, :].rearrange("p (t h) -> p t h", h=2 * H)
                nc.scalar.activation(fwd[u][:, :, 0:H], hid[:, :, 0:H], ACT.Relu).then_inc(relu_done[u], 1)
                nc.scalar.activation(bwd[u][:, :, 0:H], hid[:, :, H:2 * H], ACT.Relu).then_inc(relu_done[u], 1)
                act.wait_ge(keys_read[u], i + 1)
                nc.scalar.activation(bwd[u][:, :, H + 1], srcf[u][:, :], ACT.Copy).then_inc(relu_done[u], 1)

            def turned(i, u):
                at = bass.ds(2 * i + u, 1)
                lower = act.value_load(row_lower[0:1, at], min_val=0, max_val=NB)
                upper = act.value_load(row_upper[0:1, at], min_val=0, max_val=NB)
                if started(i):
                    act.wait_ge(hid_done[u], i)
                nc.scalar.activation(pq_win[u][0:HW, :], PQ[0:HW, bass.ds(lower * (2 * H), 2 * H)], ACT.Copy).then_inc(turned_out[u], 1)
                nc.scalar.activation(pq_win[u][HW:P, :], PQ[HW:P, bass.ds(upper * (2 * H), 2 * H)], ACT.Copy).then_inc(turned_out[u], 1)
                act.wait_ge(hot_turned[u], i + 1)
                nc.scalar.activation(hot_t[u][:, :, :].rearrange("p t e -> p (t e)"), hot_p[:, :], ACT.Copy).then_inc(turned_out[u], 1)
                act.wait_ge(ea_turned[u], i + 1)
                nc.scalar.activation(ea_t[u][:, :], ea_p[:, 0:P], ACT.Copy).then_inc(turned_out[u], 1)
                if started(i) or u:
                    relus(*before(i, u))
            turns(act, turns_of(act, loops, 0, 2), turned, relus)

        @block.tensor
        def _(pe):
            pe.wait_ge(init, INIT)
            nc.tensor.matmul(rank_p[:, 0:T * NB], ones[0:1, :], begin_row[:, :, :].rearrange("p t b -> p (t b)"),
                             start=True, stop=True, skip_group_check=True)

            def rank(i, u):
                pe.wait_ge(hot_s_ready[u], i + 1)
                hs = hot_s[u][:, :, :].rearrange("p t b -> p (t b)")
                rank_edges(nc, rank_p, hs, T, lower_b, ones_b).then_inc(ranked[u], 1)

            def complete(i, u):
                pe.wait_ge(rank_read[u], i + 1)
                hs = hot_s[u][:, :, :].rearrange("p t b -> p (t b)")
                complete_ranks(nc, rank_p, hs, T, upper_b, ones_b).then_inc(ranked[u], 1)

            def forward(i, u):
                pe.wait_ge(relu_done[u], i * 3 + 1)
                if started(i):
                    pe.wait_ge(added[u], 2 * i)
                for j in range(T):
                    last = nc.tensor.matmul(sum_p[u][0:FW, 0:P], fwd[u][:, j, :], hot[u][:, j, :], start=(j == 0), stop=(j == T - 1))
                last.then_inc(fwd_done[u], 1)

            def hidden(i, u):
                rank(i, u)
                pe.wait_ge(hot_ready[u], i + 1)
                if started(i) or u:
                    pe.wait_ge(turned_out[1 - u], 4 * before(i, u)[0] + 4)
                for j in range(T):
                    last = nc.tensor.transpose(hot_p[:, j * P:(j + 1) * P], hot[u][:, j, :], ident[:, :])
                last.then_inc(hot_turned[u], 1)
                pe.wait_ge(loaded[u], (i + 1) * 48)
                nc.tensor.transpose(ea_p[:, 0:P], ea[u][:, :, :].rearrange("p t c -> p (t c)"), ident[:, :]).then_inc(ea_turned[u], 1)
                if started(i) or u:
                    forward(*before(i, u))
                complete(i, u)
                pe.wait_ge(turned_out[u], 4 * i + 4)
                if started(i):
                    pe.wait_ge(relu_done[u], i * 3)
                nc.tensor.matmul(hid_p[u][:, :], ea_t[u][:, :], wt["wc"][:, :, :].rearrange("p t h -> p (t h)"), start=True, stop=False)
                for j in range(T):
                    nc.tensor.matmul(hid_p[u][:, j * 2 * H:(j + 1) * 2 * H], hot_t[u][:, j, :],
                                     pq_win[u][:, :], start=False, stop=False, skip_group_check=True)
                pe.wait_ge(gathered[u], (i + 1) * 16 * T)
                nc.tensor.matmul(hid_p[u][:, :], ident[:, :], qp[u][:, :, :].rearrange("p t h -> p (t h)"),
                                 start=False, stop=True).then_inc(hid_done[u], 1)
            turns(pe, turns_of(pe, loops, 0, 2), hidden, forward)


def backward_sums(nc, go, tag, bwd_dram, F, col, row_off, row_blk, less_first, loops):
    with ExitStack() as own:
        def each(name, shape, dt=FP32, make=None):
            return [own.enter_context((make or nc.sbuf_tensor)(f"{tag}_{name}{u}", shape, dt)) for u in range(BUFS)]

        sem = Semaphores(nc, own, tag)

        def sem2(name):
            return sem.each(name, BUFS)
        rows = each("rows", [P, TS, BW])
        lo = each("lo", [P, TS])
        hot = each("hot", [P, TS, P])
        sum_p = each("sum_p", [P, 512], make=nc.psum_tensor)
        loaded, lo_ready, hot_ready, sum_done, added = (sem2(n) for n in ("loaded", "lo_ready", "hot_ready", "sum_done", "added"))
        block = own.enter_context(nc.Block())

        @block.sync
        def _(sp):
            def load(i, u):
                off = sp.value_load(row_off[0:1, bass.ds(BUFS * i + u, 1)], min_val=0, max_val=E)
                if started(i):
                    sp.wait_ge(sum_done[u], i)
                    plain(sp, go)
                sp.dma_start(rows[u][:, :, :].rearrange("p t w -> p (t w)"),
                             bwd_dram[bass.ds(off, CHS), :].rearrange("(p t) w -> p (t w)", t=TS)).then_inc(loaded[u], 16)
            turns(sp, turns_of(sp, loops, 1), load, bufs=BUFS)

        @block.vector
        def _(dve):
            def add(i, u):
                b = dve.value_load(row_blk[0:1, bass.ds(BUFS * i + u, 1)], min_val=0, max_val=NB)
                dve.wait_ge(sum_done[u], i + 1)
                if started(i) or u:
                    dve.wait_ge(added[u - 1], before(i, u, BUFS)[0] + 1)
                f = F[:, bass.ds(b * P, P)]
                nc.vector.tensor_tensor(f, f, sum_p[u][0:FW, 0:P], ALU.add).then_inc(added[u], 1)

            def one_hot(i, u):
                dve.wait_ge(lo_ready[u], i + 1)
                if started(i):
                    dve.wait_ge(sum_done[u], i)
                nc.vector.tensor_tensor(hot[u][:, :, :], col[:, :].unsqueeze(1).to_broadcast([P, TS, P]),
                                        lo[u][:, :].unsqueeze(2).to_broadcast([P, TS, P]), ALU.is_equal).then_inc(hot_ready[u], 1)
                if started(i) or u >= 2:
                    add(*earlier(i, u, 2, BUFS))

            def finish(i, u):
                add(i, u - 1)
                add(i, u)
            turns(dve, turns_of(dve, loops, 1), one_hot, finish, bufs=BUFS)

        @block.scalar
        def _(act):
            def place(i, u):
                act.wait_ge(loaded[u], (i + 1) * 16)
                if started(i):
                    act.wait_ge(hot_ready[u], i)
                nc.scalar.activation(lo[u][:, :], rows[u][:, :, BW - 1], ACT.Identity,
                                     bias=less_first[:, bass.ds(BUFS * i + u, 1)]).then_inc(lo_ready[u], 1)
            turns(act, turns_of(act, loops, 1), place, bufs=BUFS)

        @block.tensor
        def _(pe):
            def sums(i, u):
                pe.wait_ge(hot_ready[u], i + 1)
                if started(i):
                    pe.wait_ge(added[u], i)
                for j in range(TS):
                    last = nc.tensor.matmul(sum_p[u][0:FW, 0:P], rows[u][:, j, 0:FW], hot[u][:, j, :], start=(j == 0), stop=(j == TS - 1))
                last.then_inc(sum_done[u], 1)
            turns(pe, turns_of(pe, loops, 1), sums, bufs=BUFS)


def node_mlp(nc, go, tag, F, X, wt):
    G = 4
    FULL = NB // (2 * G)
    SHORT = NB - FULL * 2 * G
    assert 0 < SHORT < G
    with ExitStack() as own:
        def two(name, shape, dt=FP32, make=None):
            return [own.enter_context((make or nc.sbuf_tensor)(f"{tag}_{name}{u}", shape, dt)) for u in range(2)]
        sem = Semaphores(nc, own, tag)
        flow_s, hid = two("flow_s", [H, G * P]), two("hid", [H + 1, G * P])
        flow_p, hid_p, out_p = (two(n, [P, 512], make=nc.psum_tensor) for n in ("flow_p", "hid_p", "out_p"))
        flow_done, flow_ready, hid_done, hid_ready, out_done, added = (sem.each(n) for n in (
            "flow_done", "flow_ready", "hid_done", "hid_ready", "out_done", "added"))
        one_set = sem("one_set")
        block = own.enter_context(nc.Block())

        def groups(engine, step, last=None):
            turns(engine, FULL, lambda i, u: step(i, u, G))
            step(FULL, 0, SHORT)
            if last is not None:
                last(FULL, 0, SHORT)

        @block.vector
        def _(dve):
            for u in range(2):
                nc.vector.memset(hid[u][H:H + 1, :], 1.0).then_inc(one_set, 1)

            def add(i, u, g):
                dve.wait_ge(out_done[u], i + 1)
                xb = X[:, bass.ds((2 * i + u) * (G * C), g * C)]
                nc.vector.tensor_tensor(xb.rearrange("p (g c) -> p g c", c=C), xb.rearrange("p (g c) -> p g c", c=C),
                                        out_p[u][:, 0:g * P].rearrange("p (g c) -> p g c", c=P)[:, :, 0:C], ALU.add).then_inc(added[u], 1)
            groups(dve, add)

        @block.tensor
        def _(pe):
            pe.wait_ge(one_set, 2)

            def rest(i, u, g):
                pe.wait_ge(flow_ready[u], i + 1)
                plain(pe, go)
                nc.tensor.matmul(hid_p[u][0:H, 0:g * P], wt["wn1"][:, :], flow_s[u][:, 0:g * P], start=True, stop=True).then_inc(hid_done[u], 1)
                pe.wait_ge(hid_ready[u], i + 1)
                if started(i):
                    pe.wait_ge(added[u], i)
                for n in range(g):
                    last = nc.tensor.matmul(out_p[u][:, n * P:n * P + MW], hid[u][:, n * P:(n + 1) * P], wt["wn2"][:, :], start=True, stop=True)
                last.then_inc(out_done[u], 1)

            def sums(i, u, g):
                if started(i):
                    pe.wait_ge(flow_ready[u], i)
                nc.tensor.matmul(flow_p[u][0:H, 0:g * P], wt["wf2"][:, :], F[:, bass.ds((2 * i + u) * (G * P), g * P)],
                                 start=True, stop=True).then_inc(flow_done[u], 1)
                if started(i) or u:
                    rest(*before(i, u), G)
            groups(pe, sums, rest)

        @block.scalar
        def _(act):
            def relu(i, u, g):
                act.wait_ge(hid_done[u], i + 1)
                if started(i):
                    act.wait_ge(out_done[u], i)
                nc.scalar.activation(hid[u][0:H, 0:g * P], hid_p[u][0:H, 0:g * P], ACT.Relu, bias=wt["bn1"][:, 0:1]).then_inc(hid_ready[u], 1)

            def copy(i, u, g):
                act.wait_ge(flow_done[u], i + 1)
                if started(i):
                    act.wait_ge(hid_done[u], i)
                nc.scalar.activation(flow_s[u][:, 0:g * P], flow_p[u][0:H, 0:g * P], ACT.Copy).then_inc(flow_ready[u], 1)
                if started(i) or u:
                    relu(*before(i, u), G)
            groups(act, copy, relu)


WEIGHTS = ["L0_gnn_" + n for n in ("g1", "mu1", "sigma1", "root1", "b1", "gam1", "bet1", "g2", "mu2", "sigma2", "root2",
                                   "b2", "gam2", "bet2", "gs", "mus", "sigmas", "roots", "bs", "gams", "bets")]
WEIGHTS += ["L1_gnn_" + n for n in ("Wf1", "bf1", "Wf2", "bf2", "Wn1", "bn1", "Wn2", "bn2")]


def kernel(**inputs):
    import concourse.bacc as bacc
    from concourse.bass_utils import run_bass_kernel_spmd

    nc = bacc.Bacc("TRN2", target_bir_lowering=False, num_devices=1)
    arrays, aps = {}, {}
    for name in ["x", "src", "dst", "edge_attr_16", "edge_attr_3"] + WEIGHTS:
        a = np.ascontiguousarray(inputs[name])
        arrays[f"in_{name}"] = a
        aps[name] = nc.dram_tensor(f"in_{name}", a.shape, mybir.dt.from_np(a.dtype), kind="ExternalInput").ap()
    out = nc.dram_tensor("out_x", (N, C), FP32, kind="ExternalOutput").ap()
    build(nc, aps["x"], aps["src"], aps["dst"], aps["edge_attr_16"], aps["edge_attr_3"],
          {n: aps[n] for n in WEIGHTS}, out)
    r = run_bass_kernel_spmd(nc, [arrays], core_ids=[0])
    return r.results[0]["out_x"]
```
